# Optimizing a Trainium2 kernel written in Bass

```python
import numpy as np
import jax
import jax.numpy as jnp

def _softmax(x, axis=-1):
    return jax.nn.softmax(x, axis=axis)

def _gelu(x):
    return jax.nn.gelu(x, approximate=True)

def _silu(x):
    return jax.nn.silu(x)

def _sigmoid(x):
    return jax.nn.sigmoid(x)

def _layernorm(x, axis=-1, eps=1e-05):
    m = jnp.mean(x, axis=axis, keepdims=True)
    v = jnp.var(x, axis=axis, keepdims=True)
    return (x - m) / jnp.sqrt(v + eps)

def _scatter_add(tgt, idx, src, axis=0):
    return tgt.at[idx].add(src)

def _segment_sum(src, seg, n):
    return jax.ops.segment_sum(src, seg, n)
kernel_name = 'mk_adj_preln_d4_adj_r2_d8c0f4'

def setup_inputs(seed: int=0):
    np.random.seed(seed)
    _w = jnp.asarray

    def _rec_inputs():
        import jax
        import jax.numpy as jnp
        _gk = jax.random.key(seed)
        x = -0.0002928 + 1 * jax.random.normal(jax.random.fold_in(_gk, 1), (4096, 256), jnp.float32)
        _w = (1.0 + jnp.arange(4096, dtype=jnp.float32)) ** (-0.5)
        _w = _w / _w.mean()
        _pij = jnp.clip(0.000488281 * _w[:, None] * _w[None, :], 0.0, 1.0)
        _a = jax.random.uniform(jax.random.fold_in(_gk, 2), (4096, 4096)) < _pij
        adj = _a.astype(jnp.int32)
        return (x, adj)
    x, adj = _rec_inputs()

    def _L0_gnn_setup():
        import jax, jax.numpy as jnp
        import numpy as np
        N, IN_DIM, OUT_DIM = (4096, 256, 256)
        ALPHA = 0.2
        NEG_BIG = -9000000000000000.0

        def _xavier(key, shape, gain=1.414):
            fan_in, fan_out = (shape[0], shape[1])
            bound = gain * np.sqrt(6.0 / (fan_in + fan_out))
            return jax.random.uniform(key, shape, jnp.float32, -bound, bound)
        key = jax.random.key(seed)
        k1, k2, k3, k4 = jax.random.split(key, 4)
        h = jax.random.normal(k1, (N, IN_DIM), jnp.float32)
        adj = jax.random.randint(k2, (N, N), 0, 2, jnp.int32)
        W = _xavier(k3, (IN_DIM, OUT_DIM))
        a = _xavier(k4, (2 * OUT_DIM, 1))
        return {'h': h, 'adj': adj, 'W': W, 'a': a}
    _L0_gnn_all = _L0_gnn_setup()
    _L0_gnn_in = {k: v for k, v in _L0_gnn_all.items() if k in ('W', 'a')}
    del _L0_gnn_all

    def _L1_gnn_setup():
        import jax, jax.numpy as jnp
        import numpy as np
        N, D_IN, D_OUT = (4096, 256, 256)
        key = jax.random.key(seed)
        ks = jax.random.split(key, 8)
        scale_in = 1.0 / np.sqrt(D_IN)
        scale_cat = 1.0 / np.sqrt(2 * D_OUT)
        return {'x': jax.random.normal(ks[0], (N, D_IN), dtype=jnp.float32), 'adj': jax.random.randint(ks[1], (N, N), 0, 2, dtype=jnp.int32), 'W_self': jax.random.uniform(ks[2], (D_IN, D_OUT), jnp.float32, -scale_in, scale_in), 'b_self': jax.random.uniform(ks[3], (D_OUT,), jnp.float32, -scale_in, scale_in), 'W_nb': jax.random.uniform(ks[4], (D_IN, D_OUT), jnp.float32, -scale_in, scale_in), 'b_nb': jax.random.uniform(ks[5], (D_OUT,), jnp.float32, -scale_in, scale_in), 'W_comb': jax.random.uniform(ks[6], (2 * D_OUT, D_OUT), jnp.float32, -scale_cat, scale_cat), 'b_comb': jax.random.uniform(ks[7], (D_OUT,), jnp.float32, -scale_cat, scale_cat)}
    _L1_gnn_all = _L1_gnn_setup()
    _L1_gnn_in = {k: v for k, v in _L1_gnn_all.items() if k in ('W_self', 'b_self', 'W_nb', 'b_nb', 'W_comb', 'b_comb')}
    del _L1_gnn_all

    def _L2_gnn_setup():
        import jax, jax.numpy as jnp
        import numpy as np
        B, IN_F, OUT_F, H = (1024, 256, 256, 8)
        D = OUT_F // H
        key = jax.random.key(seed)
        ks = jax.random.split(key, 4)
        x = jax.random.normal(ks[0], (B, IN_F), dtype=jnp.float32)
        W_w = jax.random.normal(ks[1], (OUT_F, IN_F), dtype=jnp.float32) * (1.0 / np.sqrt(IN_F))
        W_b = jnp.zeros((OUT_F,), dtype=jnp.float32)
        a = jax.random.normal(ks[2], (2 * D, 1), dtype=jnp.float32) * 0.1
        adj = jax.random.randint(ks[3], (B, B), 0, 2, dtype=jnp.int32)
        return {'x': x, 'adj': adj, 'W_w': W_w, 'W_b': W_b, 'a': a}
    _L2_gnn_all = _L2_gnn_setup()
    _L2_gnn_in = {k: v for k, v in _L2_gnn_all.items() if k in ('W_w', 'W_b', 'a')}
    del _L2_gnn_all

    def _L3_gnn_setup():
        import jax, jax.numpy as jnp
        import numpy as np
        N = 4096
        IN_F = 256
        OUT_F = 256
        ALPHA = 0.2
        NEG_INF = -9000000000000000.0
        key = jax.random.key(seed)
        k1, k2, k3, k4, k5 = jax.random.split(key, 5)
        x = jax.random.normal(k1, (N, IN_F), dtype=jnp.float32)
        adj = jax.random.randint(k2, (N, N), 0, 2, dtype=jnp.int32)
        W = jax.random.normal(k3, (OUT_F, IN_F), dtype=jnp.float32) / np.sqrt(IN_F)
        a1 = jax.random.normal(k4, (OUT_F,), dtype=jnp.float32) / np.sqrt(2 * OUT_F)
        a2 = jax.random.normal(k5, (OUT_F,), dtype=jnp.float32) / np.sqrt(2 * OUT_F)
        return {'x': x, 'adj': adj, 'W': W, 'a1': a1, 'a2': a2}
    _L3_gnn_all = _L3_gnn_setup()
    _L3_gnn_in = {k: v for k, v in _L3_gnn_all.items() if k in ('W', 'a1', 'a2')}
    del _L3_gnn_all
    return {'x': x, 'adj': adj, 'L0_gnn_W': _L0_gnn_in['W'], 'L0_gnn_a': _L0_gnn_in['a'], 'L1_gnn_W_self': _L1_gnn_in['W_self'], 'L1_gnn_b_self': _L1_gnn_in['b_self'], 'L1_gnn_W_nb': _L1_gnn_in['W_nb'], 'L1_gnn_b_nb': _L1_gnn_in['b_nb'], 'L1_gnn_W_comb': _L1_gnn_in['W_comb'], 'L1_gnn_b_comb': _L1_gnn_in['b_comb'], 'L2_gnn_W_w': _L2_gnn_in['W_w'], 'L2_gnn_W_b': _L2_gnn_in['W_b'], 'L2_gnn_a': _L2_gnn_in['a'], 'L3_gnn_W': _L3_gnn_in['W'], 'L3_gnn_a1': _L3_gnn_in['a1'], 'L3_gnn_a2': _L3_gnn_in['a2']}

def reference(x, adj, L0_gnn_W, L0_gnn_a, L1_gnn_W_self, L1_gnn_b_self, L1_gnn_W_nb, L1_gnn_b_nb, L1_gnn_W_comb, L1_gnn_b_comb, L2_gnn_W_w, L2_gnn_W_b, L2_gnn_a, L3_gnn_W, L3_gnn_a1, L3_gnn_a2):
    import jax
    import jax.numpy as jnp

    def _L0_gnn_ref(h, adj, W, a):
        import jax, jax.numpy as jnp
        import numpy as np
        N, IN_DIM, OUT_DIM = (4096, 256, 256)
        ALPHA = 0.2
        NEG_BIG = -9000000000000000.0

        def _xavier(key, shape, gain=1.414):
            fan_in, fan_out = (shape[0], shape[1])
            bound = gain * np.sqrt(6.0 / (fan_in + fan_out))
            return jax.random.uniform(key, shape, jnp.float32, -bound, bound)
        Wh = h @ W
        a1 = a[:OUT_DIM, 0]
        a2 = a[OUT_DIM:, 0]
        f1 = Wh @ a1
        f2 = Wh @ a2
        e = jax.nn.leaky_relu(f1[:, None] + f2[None, :], negative_slope=ALPHA)
        e = jnp.where(adj > 0, e, NEG_BIG)
        attention = jax.nn.softmax(e, axis=1)
        h_prime = attention @ Wh
        return jax.nn.elu(h_prime)

    def _L1_gnn_ref(x, adj, W_self, b_self, W_nb, b_nb, W_comb, b_comb):
        import jax, jax.numpy as jnp
        import numpy as np
        N, D_IN, D_OUT = (4096, 256, 256)
        mask = (adj > 0).astype(x.dtype)
        deg = jnp.sum(mask, axis=1, keepdims=True)
        agg = mask @ x / jnp.maximum(deg, 1.0)
        self_f = x @ W_self + b_self
        nb_f = agg @ W_nb + b_nb
        combined = jnp.concatenate([self_f, nb_f], axis=-1)
        out = combined @ W_comb + b_comb
        return jax.nn.relu(out)

    def _L2_gnn_ref(x, adj, W_w, W_b, a):
        import jax, jax.numpy as jnp
        import numpy as np
        B, IN_F, OUT_F, H = (1024, 256, 256, 8)
        D = OUT_F // H
        Bn = x.shape[0]
        h = (x @ W_w.T + W_b).reshape(Bn, H, D)
        a_src, a_dst = (a[:D, 0], a[D:, 0])
        s_src = jnp.einsum('bhd,d->bh', h, a_src)
        s_dst = jnp.einsum('bhd,d->bh', h, a_dst)
        e = jax.nn.leaky_relu(s_src[:, None, :] + s_dst[None, :, :], negative_slope=0.2)
        e = jnp.where(adj[:, :, None] == 0, jnp.float32(-1000000000.0), e)
        attn = jax.nn.softmax(e, axis=1)
        h_prime = jnp.einsum('ijh,jhd->ihd', attn, h).reshape(Bn, H * D)
        return jax.nn.elu(h_prime)

    def _L3_gnn_ref(x, adj, W, a1, a2):
        import jax, jax.numpy as jnp
        import numpy as np
        N = 4096
        IN_F = 256
        OUT_F = 256
        ALPHA = 0.2
        NEG_INF = -9000000000000000.0
        h = x @ W.T
        src = h @ a1
        dst = h @ a2
        e = jax.nn.leaky_relu(src[:, None] + dst[None, :], negative_slope=ALPHA)
        e = jnp.where(adj == 0, jnp.float32(NEG_INF), e)
        attention = jax.nn.softmax(e, axis=1)
        h_prime = attention @ h
        return h_prime
    h = jnp.maximum(_layernorm(x, axis=-1), 0.0)
    x = x + _L0_gnn_ref(h, adj, L0_gnn_W, L0_gnn_a)
    h = jnp.maximum(_layernorm(x, axis=-1), 0.0)
    x = x + _L1_gnn_ref(h, adj, L1_gnn_W_self, L1_gnn_b_self, L1_gnn_W_nb, L1_gnn_b_nb, L1_gnn_W_comb, L1_gnn_b_comb)
    h = jnp.maximum(_layernorm(x, axis=-1), 0.0)
    x = x + _L2_gnn_ref(h, adj, L2_gnn_W_w, L2_gnn_W_b, L2_gnn_a)
    h = jnp.maximum(_layernorm(x, axis=-1), 0.0)
    x = x + _L3_gnn_ref(h, adj, L3_gnn_W, L3_gnn_a1, L3_gnn_a2)
    return x

_drawn_inputs = setup_inputs


def setup_inputs(seed=0):
    import zlib

    import numpy as np

    out = dict(_drawn_inputs(seed))
    spreads = {'L2_gnn_W_b': (0.0, 0.1)}
    factors = {'L1_gnn_b_self': 7.001, 'L1_gnn_b_nb': 6.223, 'L1_gnn_b_comb': 3.722, 'L3_gnn_a1': 4.862}
    for name, (base, spread) in spreads.items():
        noise = np.random.default_rng([zlib.crc32(name.encode()), seed]).standard_normal(out[name].shape)
        drawn = base * np.exp(spread * noise) if base else spread * noise
        out[name] = jnp.asarray(drawn.astype(out[name].dtype))
    for name, factor in factors.items():
        out[name] = (out[name] * factor).astype(out[name].dtype)
    return out
```

```python
from contextlib import ExitStack

import numpy as np
import concourse.bass as bass
from concourse import mybir

ALU = mybir.AluOpType
ACT = mybir.ActivationFunctionType
AX = mybir.AxisListType
F32, BF16 = mybir.dt.float32, mybir.dt.bfloat16
I32, I16, U32 = mybir.dt.int32, mybir.dt.int16, mybir.dt.uint32
ds = bass.ds

P = 128
N = 4096
D = 256
T = N // P
JB = N // P
KC = D // P
W = 2 * P
MAXB = N // W
BIG = 1e30
FLOOR = -1e20
SLOPE = 0.2
EPS = 1e-5


class Layer:

    def __init__(self, index, heads, own, bias):
        self.index, self.heads, self.own, self.bias = index, heads, own, bias
        self.att = heads > 0
        self.sums = heads * (D // heads + 1) if heads else D + 1
        self.row = self.sums + heads
        self.cols = 2 * D if not heads else D + 2 * heads


LAYERS = [Layer(0, 1, 1, False), Layer(1, 0, D, True), Layer(2, 8, 8, True), Layer(3, 1, 1, False)]
ROW = max(l.row for l in LAYERS)
OWN = D + max(l.own for l in LAYERS)

class Sems:

    def __init__(self, nc, name):
        self.nc, self.name, self.all = nc, name, []
        self.apart = self.one("apart")
        self.vln = self.one("vln")
        self.rstd = self.one("rstd")
        self.hc = self.one("hc")
        self.hT_ps = self.one("hT_ps")
        self.hT = self.one("hT")
        self.o_ps = self.one("o_ps")
        self.o = self.one("o")
        self.hs = self.one("hs")
        self.st_tab = self.two("st_tab")
        self.st_own = self.two("st_own")
        self.xo = self.two("xo")

    def one(self, what):
        self.all.append(self.nc.alloc_semaphore(name=self.name + what))
        return self.all[-1]

    def two(self, what):
        return [self.one(f"{what}{p}") for p in range(2)]


class ListingSems(Sems):
    def __init__(self, nc, name):
        super().__init__(nc, name)
        self.const = self.one("const")
        self.ident = self.one("ident")
        self.w_in = self.one("w_in")
        self.ini = self.one("ini")
        self.wt = self.one("wt")
        self.wtc = self.one("wtc")
        self.wprod = self.one("wprod")
        self.wset = self.one("wset")
        self.v = self.one("v")
        self.flag = self.one("flag")
        self.pre = self.one("pre")
        self.rankv = self.one("rankv")
        self.base = self.one("base")
        self.mt = self.one("mt")
        self.mtc = self.one("mtc")
        self.done = self.one("done")
        self.col = self.one("col")
        self.blk_out = self.one("blk_out")
        self.cnt = self.two("cnt")
        self.onehot = self.two("onehot")
        self.picked = self.two("picked")
        self.blk = self.two("blk")
        self.indexed = self.two("indexed")
        self.x_in = self.two("x_in")
        self.mask_in = self.two("mask_in")
        self.by_pool = self.mask_in


class LayerSems(Sems):
    def __init__(self, nc, name):
        super().__init__(nc, name)
        self.yd = self.one("yd")
        self.tabs = self.one("tabs")
        self.cs_ps = self.one("cs_ps")
        self.cs = self.one("cs")
        self.mx = self.one("mx")
        self.abps = self.one("abps")
        self.ab_cp = self.one("ab_cp")
        self.y = self.one("y")
        self.ye = self.one("ye")
        self.own_in = self.two("own_in")
        self.mask_in = self.two("mask_in")
        self.acc_done = self.two("acc_done")
        self.acc_free = self.two("acc_free")
        self.idx = self.two("idx")
        self.row_cp = self.two("row_cp")
        self.z = self.two("z")
        self.zx = self.two("zx")
        self.ab = self.two("ab")
        self.low = self.two("low")
        self.t = self.two("t")
        self.nm = self.two("nm")
        self.e = self.two("e")
        self.pv = self.two("pv")
        self.row_in = self.two("row_in")
        self.by_pool = self.row_in


def build(nc, A, out):
    with ExitStack() as ctx:
        def sb(name, shape, dt=F32):
            return ctx.enter_context(nc.sbuf_tensor(name, shape, dt))

        table = [nc.dram_tensor(f"table{l.index}", [N, l.row], F32, kind="Internal").ap() for l in LAYERS]
        own_d = [nc.dram_tensor(f"own{l.index}", [N, D + l.own], F32, kind="Internal").ap() for l in LAYERS]
        block_d = nc.dram_tensor("block_masks", [(T + 1) * MAXB * P, W], BF16, kind="Internal").ap()

        identf = sb("identf", [P, P])
        identb = sb("identb", [P, 4, P], BF16)
        onesf = sb("onesf", [P, P])
        upper = sb("upper", [P, P], BF16)
        onesb = sb("onesb", [P, P], BF16)
        zrow = sb("zrow", [1, 512], BF16)
        wp = [sb(f"wp{l.index}", [P, KC, l.cols]) for l in LAYERS]
        brow = [sb(f"brow{l.index}", [1, l.cols]) if l.bias else None for l in LAYERS]
        raw = [sb(f"raw{i}", [P, KC, D]) for i in range(4)]
        rawT = [sb(f"rawT{i}", [P, KC, D]) for i in range(2)]
        comb = sb("comb", [P, 2 * KC, D])
        bcol = sb("bcol", [P, 2, KC])
        bcomb = sb("bcomb", [1, D])
        avec = [sb("avec0", [P, 2, D]), None, sb("avec2", [P, 2, 32]), sb("avec3", [P, 2, D])]
        prod = sb("prod", [P, D])
        index = sb("index", [P, 2 * (T + 1) * MAXB], I32)
        base = sb("base", [1, T + 2], I32)
        pbase = sb("pbase", [1, T + 4], I32)
        blocks = sb("blocks", [1, T], I32)
        nblkf = sb("nblkf", [1, 1])
        nblk = sb("nblk", [1, 4], I32)
        arena = sb("arena", [P, 2, MAXB * 2 * ROW])
        flat = arena[:, :, :].rearrange("p a b -> p (a b)")
        at = [0]

        def carve(words, dt, pattern=None, **k):
            v = flat[:, at[0]:at[0] + words].bitcast(dt)
            at[0] += words
            return v.rearrange(pattern, **k) if pattern else v

        MT = P + 2
        maskN = [carve(N // 2, BF16) for _ in range(2)]
        maskT = [carve(JB * MT // 2, BF16, "p (b m) -> p b m", b=JB) for _ in range(2)]
        onehot = [carve(N // 2, BF16, "p (k b) -> p k b", b=JB) for _ in range(2)]
        slots = carve(N // 2, I16, "p (k b) -> p k b", b=JB)
        assert at[0] <= 2 * MAXB * 2 * ROW
        flag = sb("flag", [P, JB], BF16)
        cum = sb("cum", [P, JB])
        rank = sb("rank", [P, JB])
        rank16 = sb("rank16", [P, 2, JB], I16)
        place32 = sb("place32", [P, JB, 2], I32)
        block = [sb(f"block{c}", [P, P], BF16) for c in range(2)]
        own = [sb(f"own_{p}", [P, OWN]) for p in range(2)]
        xo = [sb(f"xo_{p}", [P, OWN]) for p in range(2)]
        tab = [sb(f"tab_{p}", [P, ROW]) for p in range(2)]
        masks = [sb(f"masks_{p}", [P, MAXB, W], BF16) for p in range(2)]
        rows = [sb(f"rows_{c}", [P, ROW]) for c in range(2)]
        idx = [sb(f"idx_{c}", [P, 1], I32) for c in range(2)]
        scmax = [sb(f"scmax_{p}", [P, 8, 2 * MAXB]) for p in range(2)]
        small = sb("small", [P, 6, 8])
        ab = [sb(f"ab_{p}", [P, 2, 8]) for p in range(2)]
        none = [sb(f"none_{p}", [P, P]) for p in range(2)]
        abB = [sb(f"abB_{p}", [P, 2, 8, P]) for p in range(2)]
        low = [sb(f"low_{c}", [P, 8, P]) for c in range(2)]
        score = [sb(f"score_{c}", [P, 8, P]) for c in range(2)]
        prob = [sb(f"prob_{c}", [P, 8, P]) for c in range(2)]
        mask32 = [sb(f"mask32_{c}", [P, P]) for c in range(2)]
        hsum = sb("hsum", [P, ROW])
        csum = sb("csum", [P, ROW])
        stats = sb("stats", [P, 6])
        mv = sb("mv", [P, 2])
        veps = sb("veps", [P, 1])
        mhalf = sb("mhalf", [P, 1])
        rstd = sb("rstd", [P, 1])
        hc = sb("hc", [P, D])
        hT = sb("hT", [P, KC, P])
        den = sb("den", [P, 8])
        y = sb("y", [P, D])
        yneg = sb("yneg", [P, D])
        bank = [ctx.enter_context(nc.psum_tensor(f"bank{i}", [P, 512], F32)) for i in range(8)]
        z = [bank[0:2], bank[2:4]]
        acc = bank[4:6]
        tpb, opb = bank[6], bank[7]
        tb16 = [bank[i][:, :].bitcast(BF16).rearrange("p (b i) -> p b i", b=8) for i in range(2)]
        counts, ranks, picked = bank[4], bank[5], bank[2:4]

        def tiles(eng, ahead, main, late=None):
            ahead(0, 0, 0)
            if late:
                late(0, 0, 0)
            with eng.Fori(0, T // 2 - 1) as j:
                for t, p, i in ((j * 2, 0, j), (j * 2 + 1, 1, j)):
                    nxt = (t + 1, 1 - p, j + p)
                    ahead(*nxt)
                    main(t, p, i)
                    if late:
                        late(*nxt)
            ahead(T - 1, 1, T // 2 - 1)
            main(T - 2, 0, T // 2 - 1)
            if late:
                late(T - 1, 1, T // 2 - 1)
            main(T - 1, 1, T // 2 - 1)

        def load(eng, tensor, at_, lo, hi):
            return eng.value_load(tensor[0:1, ds(at_, 1)], min_val=lo, max_val=hi)

        def apart(eng, S):
            eng.sem_inc(S.apart, 1)

        def blocks_of(eng, t):
            return load(eng, base, t, 0, T * MAXB - 1), load(eng, blocks, t, 1, MAXB)

        def rows_of(ap, t):
            return ap[ds(t * P, P), :]


        def stores(sp, S, l, t, p, i):
            sp.wait_ge(S.o, t + 2)
            apart(sp, S)
            sp.dma_start(rows_of(table[l.index], t), tab[p][:, 0:l.row]).then_inc(S.st_tab[p], 16)
            sp.dma_start(rows_of(own_d[l.index], t), xo[p][:, 0:D + l.own]).then_inc(S.st_own[p], 16)

        def root(pool, S, t):
            pool.wait_ge(S.vln, t * 3 + 3 + 1)
            nc.gpsimd.tensor_tensor(rstd[:, :], veps[:, :], mhalf[:, :], ALU.pow).then_inc(S.rstd, 1)

        def add_up(pool, S, l, t, p):
            pool.wait_ge(S.o, t + 2)
            pool.wait_ge(S.hs, t + 2)
            nc.gpsimd.tensor_tensor(hsum[:, 0:l.sums], hsum[:, 0:l.sums], tab[p][:, 0:l.sums], ALU.add)\
              .then_inc(S.hs, 1)

        def project(pe, S, l, t, p, i):
            pe.wait_ge(S.hc, t + 2)
            pe.wait_ge(S.hT, t + 1)
            for k in range(KC):
                last = nc.tensor.transpose(tpb[:, k * P:(k + 1) * P], hc[:, k * P:(k + 1) * P], identf[:, :])
            last.then_inc(S.hT_ps, 1)
            pe.wait_ge(S.hT, t + 2)
            pe.wait_ge(S.o, t + 1)
            o = opb[:, 0:l.cols]
            for k in range(KC):
                last = nc.tensor.matmul(o, hT[:, k, :], wp[l.index][:, k, :], start=(k == 0),
                                        stop=(k == KC - 1 and not l.bias))
            if l.bias:
                last = nc.tensor.matmul(o, onesf[0:1, :], brow[l.index][:, :], start=False, stop=True)
            last.then_inc(S.o_ps, 1)

        def project_out(act, S, l, t, p, i):
            H = l.heads
            act.wait_ge(S.hT_ps, t + 2)
            act.wait_ge(S.o_ps, t + 1)
            nc.scalar.activation(hT[:, :, :].rearrange("p k i -> p (k i)"), tpb[:, 0:D], ACT.Relu)\
              .then_inc(S.hT, 1)
            act.wait_ge(S.o_ps, t + 2)
            act.wait_ge(S.st_tab[p], i * 16 + 1)
            if l.att:
                F = D // H
                dst = tab[p][:, 0:l.sums].rearrange("p (h f) -> p h f", h=H)[:, :, 0:F]
                nc.scalar.copy(dst, opb[:, 0:D].rearrange("p (h f) -> p h f", h=H))
                nc.scalar.copy(tab[p][:, l.sums:l.row], opb[:, D:D + H])
                nc.scalar.copy(xo[p][:, D:D + H], opb[:, D + H:D + 2 * H]).then_inc(S.o, 1)
            else:
                nc.scalar.copy(tab[p][:, 0:D], opb[:, 0:D])
                nc.scalar.copy(xo[p][:, D:2 * D], opb[:, D:2 * D]).then_inc(S.o, 1)

        def norm(dve, S, l, t, p, i):
            x = xo[p][:, 0:D]
            nc.vector.bn_stats(stats[:, :], x).then_inc(S.vln, 1)
            dve.wait_ge(S.vln, t * 3 + 2)
            apart(dve, S)
            nc.vector.bn_aggr(mv[:, :], stats[:, :]).then_inc(S.vln, 1)
            dve.wait_ge(S.vln, t * 3 + 2 + 1)
            nc.vector.tensor_scalar(veps[:, :], mv[:, 1:2], EPS, None, ALU.add).then_inc(S.vln, 1)
            dve.wait_ge(S.rstd, t + 2)
            dve.wait_ge(S.hT_ps, t + 1)
            nc.vector.tensor_scalar(hc[:, :], x, mv[:, 0:1], rstd[:, 0:1], ALU.subtract, ALU.mult)\
              .then_inc(S.hc, 1)


        def listing(blk, S):
            @blk.sync
            def _(sp):
                def w_in(dst, src):
                    sp.dma_start(dst, src).then_inc(S.w_in, 16)
                w_in(wp[0][:, :, 0:D], A["L0_gnn_W"].rearrange("(c p) n -> p c n", p=P))
                for i, n in enumerate(("L1_gnn_W_self", "L1_gnn_W_nb", "L2_gnn_W_w", "L3_gnn_W")):
                    w_in(raw[i][:, :, :], A[n].rearrange("(c p) n -> p c n", p=P))
                w_in(comb[:, :, :], A["L1_gnn_W_comb"].rearrange("(c p) n -> p c n", p=P))
                w_in(avec[0][:, :, :].rearrange("p a d -> p (a d)"),
                     A["L0_gnn_a"].rearrange("d a -> (a d)").partition_broadcast(P))
                w_in(avec[2][:, :, :].rearrange("p a d -> p (a d)"),
                     A["L2_gnn_a"].rearrange("d a -> (a d)").partition_broadcast(P))
                w_in(avec[3][:, 0, :], A["L3_gnn_a1"].partition_broadcast(P))
                w_in(avec[3][:, 1, :], A["L3_gnn_a2"].partition_broadcast(P))
                with nc.allow_non_contiguous_dma(reason="two short columns"):
                    w_in(bcol[:, 0, :], A["L1_gnn_b_self"].rearrange("(c p) -> p c", p=P))
                    w_in(bcol[:, 1, :], A["L1_gnn_b_nb"].rearrange("(c p) -> p c", p=P))
                w_in(bcomb[:, :], A["L1_gnn_b_comb"].rearrange("(a d) -> a d", a=1))
                w_in(brow[2][:, 0:D], A["L2_gnn_W_b"].rearrange("(a d) -> a d", a=1))

                def ahead(t, p, i):
                    sp.wait_ge(S.st_own[p], i * 16 + 1)
                    sp.dma_start(xo[p][:, 0:D], rows_of(A["x"], t)).then_inc(S.x_in[p], 16)

                def main(t, p, i):
                    sp.wait_ge(S.base, t + 2)
                    first, count = blocks_of(sp, t)
                    with sp.Fori(0, count) as b:
                        g = first + b
                        for c in range(2):
                            sp.wait_ge(S.blk[c], g + 2)
                        for c in range(2):
                            sp.dma_start(block_d[ds(g * P, P), c * P:(c + 1) * P], block[c][:, :])\
                              .then_inc(S.blk_out, 16)
                    sp.wait_ge(S.o, t + 2)
                    sp.dma_start(rows_of(table[0], t), tab[p][:, 0:LAYERS[0].row]).then_inc(S.st_tab[p], 16)
                    sp.dma_start(rows_of(own_d[0], t), xo[p][:, 0:D + 1]).then_inc(S.st_own[p], 16)

                tiles(sp, ahead, main)
                total = load(sp, base, T, 1, T * MAXB)
                sp.wait_ge(S.blk_out, total * 32 + 1)
                apart(sp, S)
                for p in range(2):
                    sp.wait_ge(S.st_tab[p], 16 * T // 2 + 1)
                    sp.wait_ge(S.st_own[p], 16 * T // 2 + 1)


            @blk.gpsimd
            def _(pool):
                nc.gpsimd.memset(identf[:, :], 0.0).then_inc(S.const, 1)
                nc.gpsimd.memset(upper[:, :], 1.0).then_inc(S.const, 1)
                nc.gpsimd.iota(slots, [[1, P], [0, JB]], base=0, channel_multiplier=0).then_inc(S.ident, 1)
                nc.gpsimd.iota(place32[:, :, 0], [[1, JB]], base=0, channel_multiplier=0).then_inc(S.ident, 1)
                nc.gpsimd.iota(place32[:, :, 1], [[0, JB]], base=0, channel_multiplier=1).then_inc(S.ident, 1)
                pool.wait_ge(S.const, 2 + 1)
                nc.gpsimd.affine_select(out=identf[:, :], in_=identf[:, :], compare_op=ALU.not_equal, fill=1.0,
                                        base=0, pattern=[[-1, P]], channel_multiplier=1).then_inc(S.ident, 1)
                nc.gpsimd.affine_select(out=upper[:, :], in_=upper[:, :], compare_op=ALU.is_ge, fill=0.0,
                                        base=0, pattern=[[1, P]], channel_multiplier=-1).then_inc(S.ident, 1)
                nc.gpsimd.memset(hsum[:, :], 0.0).then_inc(S.hs, 1)

                def ahead(t, p, i):
                    pool.wait_ge(S.cnt[p], i + 1)
                    pool.dma_start(maskN[p], rows_of(A["adj"], t)).then_inc(S.mask_in[p], 16)

                def main(t, p, i):
                    root(pool, S, t)
                    add_up(pool, S, LAYERS[0], t, p)

                tiles(pool, ahead, main)
                pool.wait_ge(S.base, T + 1)


            @blk.tensor
            def _(pe):
                pe.wait_ge(S.ident, 5 + 1)
                pe.wait_ge(S.w_in, 16 * 14 + 1)
                for i in range(4):
                    for cc in range(KC):
                        for rc in range(KC):
                            k = cc * KC + rc
                            last = nc.tensor.transpose(bank[i][:, k * P:(k + 1) * P],
                                                       raw[i][:, rc, cc * P:(cc + 1) * P], identf[:, :])
                    last.then_inc(S.wt, 1)
                pe.wait_ge(S.wtc, 2 + 1)
                for which, off in ((1, KC), (0, 0)):
                    for kc in range(KC):
                        o = bank[4 + which][:, kc * D:(kc + 1) * D]
                        for mc in range(KC):
                            last = nc.tensor.matmul(o, rawT[which][:, mc, kc * P:(kc + 1) * P], comb[:, off + mc, :],
                                                    start=(mc == 0), stop=(mc == KC - 1))
                    last.then_inc(S.wprod, 1)
                pe.wait_ge(S.ini, 2 + 1)
                for s in range(2):
                    for mc in range(KC):
                        nc.tensor.matmul(bank[6][0:1, 0:D], bcol[:, s, mc:mc + 1], comb[:, KC * s + mc, :],
                                         start=(s == 0 and mc == 0), stop=False)
                nc.tensor.matmul(bank[6][0:1, 0:D], onesf[0:1, 0:1], bcomb[:, :], start=False, stop=True)\
                  .then_inc(S.wprod, 1)
                pe.wait_ge(S.wset, 1 + 1)

                def ahead(t, p, i):
                    pe.wait_ge(S.mask_in[p], 16 * (i + 1))
                    for q in range(4):
                        pe.wait_ge(S.mtc, t * 4 + max(q - 1, 0) + 1)
                        for b in range(8):
                            jb = 8 * q + b
                            last = nc.tensor.transpose(tb16[q % 2][:, b, :], maskN[p][:, jb * P:(jb + 1) * P],
                                                       identb[:, 0, :])
                        last.then_inc(S.mt, 1)
                    pe.wait_ge(S.flag, t + 1)
                    for jb in range(JB):
                        last = nc.tensor.matmul(counts[:, jb:jb + 1], maskN[p][:, jb * P:(jb + 1) * P],
                                                onesb[:, 0:1], start=True, stop=True)
                    last.then_inc(S.cnt[p], 1)
                    pe.wait_ge(S.flag, t + 2)
                    pe.wait_ge(S.base, t + 1)
                    nc.tensor.matmul(ranks[:, 0:JB], upper[:, :], flag[:, :], start=True, stop=True)
                    nc.tensor.matmul(ranks[:, JB:2 * JB], onesb[:, :], flag[:, :], start=True, stop=True)\
                      .then_inc(S.pre, 1)

                def main(t, p, i):
                    pe.wait_ge(S.base, t + 2)
                    first, count = blocks_of(pe, t)
                    pe.wait_ge(S.mtc, t * 4 + 4 + 1)
                    apart(pe, S)
                    with pe.Fori(0, count) as b:
                        g = first + b
                        for c in range(2):
                            pe.wait_ge(S.onehot[c], g + 2)
                            pe.wait_ge(S.blk[c], g + 1)
                            pe.wait_ge(S.indexed[c], g + 1)
                            for jb in range(JB):
                                mm = nc.tensor.matmul(picked[c][:, 0:MT], onehot[c][:, :, jb], maskT[p][:, jb, :],
                                                      start=(jb == 0), stop=(jb == JB - 1))
                            mm.then_inc(S.picked[c], 1)
                    project(pe, S, LAYERS[0], t, p, i)

                tiles(pe, ahead, main)


            @blk.scalar
            def _(act):
                act.wait_ge(S.wset, 1 + 1)

                def ahead(t, p, i):
                    for q in range(4):
                        act.wait_ge(S.mt, t * 4 + q + 2)
                        nc.scalar.copy(maskT[p][:, 8 * q:8 * q + 8, 0:P], tb16[q % 2]).then_inc(S.mtc, 1)

                def main(t, p, i):
                    act.wait_ge(S.base, t + 2)
                    first, count = blocks_of(act, t)
                    with act.Fori(0, count) as b:
                        g = first + b
                        act.wait_ge(S.blk_out, g * 32 + 1)
                        for c in range(2):
                            act.wait_ge(S.picked[c], g + 2)
                            nc.scalar.activation(block[c][:, :], picked[c][:, 0:P], ACT.Copy, scale=BIG, bias=-BIG)\
                              .then_inc(S.blk[c], 1)
                    project_out(act, S, LAYERS[0], t, p, i)

                tiles(act, ahead, main)


            @blk.vector
            def _(dve):
                V = [0]

                def link(ins):
                    V[0] += 1
                    ins.then_inc(S.v, 1)
                    dve.wait_ge(S.v, V[0] + 1)

                nc.vector.memset(onesf[:, :], 1.0).then_inc(S.ini, 1)
                nc.vector.memset(mhalf[:, :], -0.5)
                nc.vector.memset(zrow[:, :], 0.0)
                nc.vector.memset(base[:, :], 0)
                nc.vector.memset(pbase[:, :], 0)
                for p in range(2):
                    nc.vector.memset(tab[p][:, :], 1.0)
                nc.vector.memset(brow[1][:, 0:D], 0.0)
                link(nc.vector.memset(onesb[:, :], 1.0))
                nc.vector.memset(none[0][:, :], 0.0).then_inc(S.ini, 1)
                dve.wait_ge(S.ident, 5 + 1)
                link(nc.vector.tensor_copy(identb[:, :, :], identf[:, :].unsqueeze(1).to_broadcast([P, 4, P])))
                for p in range(2):
                    link(nc.vector.tensor_copy(maskT[p][:, :, P:P + 2], place32[:, :, :]))
                for i, dst in enumerate((rawT[0][:, :, :], rawT[1][:, :, :], wp[2][:, :, 0:D], wp[3][:, :, 0:D])):
                    dve.wait_ge(S.wt, i + 2)
                    ins = nc.vector.tensor_copy(dst, bank[i][:, :].rearrange("p (k n) -> p k n", k=KC))
                    if i < 2:
                        ins.then_inc(S.wtc, 1)
                    else:
                        link(ins)
                for n, which in enumerate((1, 0)):
                    dve.wait_ge(S.wprod, n + 2)
                    link(nc.vector.tensor_copy(wp[1][:, :, n * D:(n + 1) * D],
                                               bank[4 + which][:, :].rearrange("p (k n) -> p k n", k=KC)))
                dve.wait_ge(S.wprod, 3 + 1)
                link(nc.vector.tensor_copy(brow[1][:, D:2 * D], bank[6][0:1, 0:D]))
                dve.wait_ge(S.w_in, 16 * 14 + 1)
                for l in (LAYERS[0], LAYERS[2], LAYERS[3]):
                    H, F = l.heads, D // l.heads
                    srcs = [wp[l.index][:, k, :] for k in range(KC)] + ([brow[2][:, :]] if l.bias else [])
                    for w in srcs:
                        n = w.shape[0]
                        for s in range(2):
                            pv = prod[0:n, :].rearrange("p (h f) -> p h f", h=H)
                            av = avec[l.index][0:n, 1 - s, :].unsqueeze(1).to_broadcast([n, H, F])
                            link(nc.vector.tensor_tensor(pv, w[:, 0:D].rearrange("p (h f) -> p h f", h=H), av, ALU.mult))
                            link(nc.vector.tensor_reduce(w[:, D + s * H:D + s * H + H], pv, AX.X, ALU.add))
                nc.vector.memset(scmax[0][:, :, :], -BIG).then_inc(S.wset, 1)

                R = 7

                def ahead(t, p, i):
                    dve.wait_ge(S.cnt[p], i + 2)
                    dve.wait_ge(S.pre, t + 1)
                    nc.vector.tensor_scalar(flag[:, :], counts[:, 0:JB], 0.0, None, ALU.is_gt).then_inc(S.flag, 1)

                def ranking(t, p, i):
                    dve.wait_ge(S.pre, t + 2)
                    k = [0]

                    def step(ins):
                        k[0] += 1
                        ins.then_inc(S.rankv, 1)
                        dve.wait_ge(S.rankv, t * R + k[0] + 1)

                    tot = ranks[:, JB:2 * JB]
                    step(nc.vector.tensor_tensor_scan(cum[:, :], onesf[:, 0:JB], tot, 0.0, ALU.mult, ALU.add))
                    step(nc.vector.tensor_scalar(nblk[:, 0:1], cum[0:1, JB - 1:JB], float(W - 1), None, ALU.add))
                    step(nc.vector.tensor_scalar(nblk[:, 1:2], nblk[:, 0:1], 8, None, ALU.arith_shift_right))
                    step(nc.vector.tensor_scalar(nblkf[:, :], nblk[:, 1:2], 1.0, None, ALU.max))
                    nc.vector.tensor_copy(blocks[:, ds(t, 1)], nblkf[:, :])
                    nc.vector.tensor_tensor(base[:, ds(t + 1, 1)], base[:, ds(t, 1)], nblkf[:, :], ALU.add)
                    nc.vector.tensor_tensor(pbase[:, ds(t + 2, 1)], pbase[:, ds(t, 1)], nblkf[:, :], ALU.add)
                    step(nc.vector.scalar_tensor_tensor(rank[:, :], ranks[:, 0:JB], 2.0 * N - 1, cum[:, :],
                                                        ALU.add, ALU.add))
                    step(nc.vector.tensor_tensor(rank[:, :], rank[:, :], tot, ALU.subtract))
                    step(nc.vector.tensor_tensor(rank[:, :], rank[:, :], flag[:, :], ALU.mult))
                    assert k[0] == R
                    for c in range(2):
                        ins = nc.vector.tensor_scalar(rank16[:, c, :], rank[:, :], -2.0 * N - c * P, None, ALU.add)
                    ins.then_inc(S.base, 1)

                def main(t, p, i):
                    dve.wait_ge(S.base, t + 2)
                    apart(dve, S)
                    first, count = blocks_of(dve, t)
                    with dve.Fori(0, count) as b:
                        g = first + b
                        for c in range(2):
                            dve.wait_ge(S.picked[c], g + 1)
                            dve.wait_ge(S.done, g * 2 + 1)
                            nc.vector.tensor_tensor(onehot[c], slots,
                                                    rank16[:, c, :].unsqueeze(1).to_broadcast([P, P, JB]),
                                                    ALU.is_equal).then_inc(S.onehot[c], 1)
                        for c in range(2):
                            dve.wait_ge(S.onehot[c], g + 2)
                            nc.vector.tensor_scalar(rank16[:, c, :], rank16[:, c, :], float(W), None, ALU.subtract)\
                              .then_inc(S.done, 1)
                        for c in range(2):
                            dve.wait_ge(S.picked[c], g + 2)
                            dve.wait_ge(S.blk[c], g + 2)
                            nc.vector.tensor_scalar(rank[:, c:c + 1], picked[c][:, P:P + 1], float(P), None, ALU.mult)\
                              .then_inc(S.col, 1)
                            dve.wait_ge(S.col, g * 2 + c + 2)
                            nc.vector.tensor_tensor(index[:, ds(g * 2 + c, 1)], rank[:, c:c + 1],
                                                    picked[c][:, P + 1:P + 2], ALU.add).then_inc(S.indexed[c], 1)
                    dve.wait_ge(S.x_in[p], 16 * (i + 1) + 1)
                    norm(dve, S, LAYERS[0], t, p, i)

                def late(t, p, i):
                    ranking(t, p, i)

                tiles(dve, ahead, main, late)



        def layer(blk, l, nxt, S):
            @blk.sync
            def _(sp):

                def ahead(t, p, i):
                    first, count = blocks_of(sp, t)
                    sp.wait_ge(S.xo[p], i + 1)
                    sp.dma_start(own[p][:, 0:D + l.own], rows_of(own_d[l.index], t)).then_inc(S.own_in[p], 16)
                    sp.wait_ge(S.acc_done[p], i + 1)
                    apart(sp, S)
                    with sp.Fori(0, count) as b:
                        g = first + b
                        sp.dma_start(masks[p][:, ds(b, 1), :].rearrange("q a w -> q (a w)"),
                                     block_d[ds(g * P, P), :]).then_inc(S.mask_in[p], 16)

                def main(t, p, i):
                    if nxt:
                        stores(sp, S, nxt, t, p, i)
                    else:
                        sp.wait_ge(S.xo[p], i + 2)
                        apart(sp, S)
                        sp.dma_start(rows_of(out, t), xo[p][:, 0:D]).then_inc(S.st_own[p], 16)

                tiles(sp, ahead, main)
                for p in range(2):
                    if nxt:
                        sp.wait_ge(S.st_tab[p], 16 * T // 2 + 1)
                    sp.wait_ge(S.st_own[p], 16 * T // 2 + 1)

            @blk.gpsimd
            def _(pool):
                if nxt and nxt.att:
                    if l.att:
                        pool.wait_ge(S.cs_ps, 1 + 1)
                    nc.gpsimd.memset(hsum[:, :], 0.0).then_inc(S.hs, 1)

                def gather(t, p, i):
                    first, count = blocks_of(pool, t)
                    with pool.Fori(0, count) as b:
                        g = first + b
                        for c in range(2):
                            pool.wait_ge(S.row_cp[c], g + 1)
                            nc.gpsimd.tensor_copy(idx[c][:, :], index[:, ds(g * 2 + c, 1)]).then_inc(S.idx[c], 1)
                        for c in range(2):
                            pool.wait_ge(S.idx[c], g + 2)
                            if l.att:
                                pool.wait_ge(S.z[c], g + 1)
                            apart(pool, S)
                            nc.gpsimd.indirect_dma_start(
                                rows[c][:, 0:l.row], None, table[l.index][:, :],
                                bass.IndirectOffsetOnAxis(idx[c][:, :].bitcast(U32), 0)).then_inc(S.row_in[c], 16)

                def mask_add(t, p, i):
                    if l.att:
                        first, count = blocks_of(pool, t)
                        with pool.Fori(0, count) as b:
                            g = first + b
                            for c in range(2):
                                pool.wait_ge(S.t[c], g + 2)
                                sc = score[c][:, 0:l.heads, :]
                                m = masks[p][:, ds(b, 1), c * P:(c + 1) * P]
                                nc.gpsimd.tensor_tensor(sc, sc, m.to_broadcast([P, l.heads, P]), ALU.add)\
                                  .then_inc(S.nm[c], 1)
                    if nxt:
                        root(pool, S, t)
                    if nxt and nxt.att:
                        add_up(pool, S, nxt, t, p)

                tiles(pool, gather, mask_add)

            @blk.tensor
            def _(pe):
                H = l.heads
                if l.att:
                    nc.tensor.matmul(opb[:, 0:l.sums], onesf[:, :], hsum[:, 0:l.sums], start=True, stop=True)\
                      .then_inc(S.cs_ps, 1)
                    pe.wait_ge(S.cs, 1 + 1)

                def spread(t, p, i):
                    if not l.att:
                        return
                    first, count = blocks_of(pe, t)
                    par = load(pe, pbase, t + 2, 1, T * MAXB)
                    pe.wait_ge(S.mask_in[p], par * 16 + 1)
                    pe.wait_ge(S.ab_cp, t + 1)
                    apart(pe, S)
                    hb = min(H, 4)
                    with pe.Fori(0, count) as b:
                        g = first + b
                        for c in range(2):
                            pe.wait_ge(S.row_in[c], g * 16 + 16)
                            pe.wait_ge(S.zx[c], g + 1)
                            m = masks[p][:, ds(b, 1), c * P:(c + 1) * P].rearrange("q a w -> q (a w)")
                            for h in range(0, H, 4):
                                o = z[c][h // 4]
                                nc.tensor.matmul(o[:, 0:hb * P], m,
                                                 identb[:, 0:hb, :].rearrange("p a b -> p (a b)"),
                                                 start=True, stop=False)
                                for k in range(hb):
                                    s = l.sums + h + k
                                    last_mm = nc.tensor.matmul(
                                        o[:, k * P:(k + 1) * P], rows[c][:, s:s + 1].to_broadcast([P, P]),
                                        identf[:, :], start=False, stop=(k == hb - 1))
                            last_mm.then_inc(S.z[c], 1)

                def weigh(t, p, i):
                    first, count = blocks_of(pe, t)
                    a = acc[p]
                    F = D // H + 1 if H else l.row
                    pe.wait_ge(S.acc_free[p], i + 1)
                    nc.tensor.matmul(a[:, 0:l.sums], zrow[:, 0:P], zrow[:, 0:l.sums], start=True, stop=False)
                    with pe.Fori(0, count) as b:
                        g = first + b
                        for c in range(2):
                            pe.wait_ge(S.e[c], g + 2)
                            pe.wait_ge(S.row_cp[c], g + 2)
                            for h in range(max(H, 1)):
                                r = arena[:, p, ds(b * (2 * ROW) + (c * ROW + h * F), F)]
                                wt = prob[c][:, h, :] if l.att else mask32[c][:, :]
                                mm = nc.tensor.matmul(a[:, h * F:(h + 1) * F], wt, r, start=False, stop=False)
                            mm.then_inc(S.pv[c], 1)
                    if l.att:
                        nc.tensor.matmul(a[:, 0:l.sums], none[p][:, :], csum[:, 0:l.sums], start=False,
                                         stop=True).then_inc(S.acc_done[p], 1)
                    else:
                        nc.tensor.matmul(a[:, 0:l.sums], zrow[:, 0:P], zrow[:, 0:l.sums], start=False,
                                         stop=True).then_inc(S.acc_done[p], 1)

                def main(t, p, i):
                    weigh(t, p, i)
                    if nxt:
                        project(pe, S, nxt, t, p, i)

                def late(t, p, i):
                    pe.wait_ge(S.ab[p], i + 2)
                    for v in range(2):
                        for h in range(H):
                            mm = nc.tensor.matmul(z[v][h // 4][:, (h % 4) * P:(h % 4 + 1) * P],
                                                  ab[p][:, v, h:h + 1].to_broadcast([P, P]), identf[:, :],
                                                  start=(h % 4 == 0), stop=(h % 4 == 3 or h == H - 1),
                                                  skip_group_check=True)
                    mm.then_inc(S.abps, 1)

                tiles(pe, spread, main, late if l.att else None)

            @blk.scalar
            def _(act):
                H = l.heads
                if nxt:
                    act.wait_ge(S.tabs, 1 + 1)

                def keep(t, p, i):
                    first, count = blocks_of(act, t)
                    act.wait_ge(S.acc_done[p], i + 1)
                    apart(act, S)
                    with act.Fori(0, count) as b:
                        g = first + b
                        for c in range(2):
                            act.wait_ge(S.row_in[c], g * 16 + 16)
                            nc.scalar.copy(arena[:, p, ds(b * (2 * ROW) + c * ROW, l.row)],
                                           rows[c][:, 0:l.row]).then_inc(S.row_cp[c], 1)

                def main(t, p, i):
                    if l.att:
                        first, count = blocks_of(act, t)
                        with act.Fori(0, count) as b:
                            g = first + b
                            for c in range(2):
                                act.wait_ge(S.nm[c], g + 2)
                                act.wait_ge(S.pv[c], g + 1)
                                nc.scalar.activation(prob[c][:, 0:H, :], score[c][:, 0:H, :], ACT.Exp)\
                                  .then_inc(S.e[c], 1)
                    if l.index in (0, 2):
                        act.wait_ge(S.y, t + 2)
                        nc.scalar.activation(yneg[:, :], yneg[:, :], ACT.Exp).then_inc(S.ye, 1)
                    if nxt:
                        project_out(act, S, nxt, t, p, i)

                def late(t, p, i):
                    act.wait_ge(S.abps, t + 2)
                    act.wait_ge(S.xo[p], i + 1)
                    for v in range(2):
                        for h in range(0, H, 4):
                            n = min(4, H)
                            mm = nc.scalar.copy(abB[p][:, v, h:h + n, :].rearrange("p h i -> p (h i)"),
                                                z[v][h // 4][:, 0:n * P])
                    mm.then_inc(S.ab_cp, 1)

                tiles(act, keep, main, late if l.att else None)

            @blk.vector
            def _(dve):
                H = l.heads
                for p in range(2):
                    ins = nc.vector.memset(tab[p][:, :], 1.0)
                ins.then_inc(S.tabs, 1)
                if l.att:
                    dve.wait_ge(S.cs_ps, 1 + 1)
                    nc.vector.tensor_copy(csum[:, 0:l.sums], opb[:, 0:l.sums]).then_inc(S.cs, 1)
                MX = 7

                def maxima(t, p, i):
                    if not l.att:
                        return
                    first, count = blocks_of(dve, t)
                    k = [0]

                    def step(ins):
                        k[0] += 1
                        ins.then_inc(S.mx, 1)
                        dve.wait_ge(S.mx, t * MX + k[0] + 1)

                    step(nc.vector.memset(scmax[p][:, 0:H, :], -BIG))
                    apart(dve, S)
                    with dve.Fori(0, count) as b:
                        g = first + b
                        for c in range(2):
                            dve.wait_ge(S.z[c], g + 2)
                            for h in range(0, H, 4):
                                n = min(4, H)
                                ins = nc.vector.tensor_reduce(
                                    scmax[p][:, h:h + n, ds(b * 2 + c, 1)],
                                    z[c][h // 4][:, 0:n * P].rearrange("p (h i) -> p h i", h=n), AX.X, ALU.max)
                            ins.then_inc(S.zx[c], 1)
                    for c in range(2):
                        dve.wait_ge(S.zx[c], first + count + 1)
                    zm, s, m = small[:, 0, 0:H], small[:, 1, 0:H], small[:, 2, 0:H]
                    step(nc.vector.tensor_reduce(zm, scmax[p][:, 0:H, :], AX.X, ALU.max))
                    dve.wait_ge(S.own_in[p], 16 * (i + 1) + 1)
                    dve.wait_ge(S.abps, t + 1)
                    f1 = own[p][:, D:D + H]
                    step(nc.vector.tensor_tensor(s, f1, zm, ALU.add))
                    step(nc.vector.scalar_tensor_tensor(m, s, SLOPE, s, ALU.mult, ALU.max))
                    step(nc.vector.tensor_scalar(s, m, FLOOR, None, ALU.max))
                    nc.vector.tensor_tensor(ab[p][:, 0, 0:H], f1, s, ALU.subtract)
                    step(nc.vector.scalar_tensor_tensor(ab[p][:, 1, 0:H], s, -1.0 / SLOPE, f1, ALU.mult, ALU.add))
                    step(nc.vector.tensor_scalar(small[:, 3, 0:1], zm[:, 0:1], -0.1 * BIG, None, ALU.is_lt))
                    assert k[0] == MX
                    nc.vector.tensor_scalar(none[p][:, :], identf[:, :], small[:, 3, 0:1], None, ALU.mult)\
                      .then_inc(S.ab[p], 1)

                def scores(t, p, i):
                    first, count = blocks_of(dve, t)
                    if l.att:
                        dve.wait_ge(S.ab_cp, t + 2)
                        apart(dve, S)
                        with dve.Fori(0, count) as b:
                            g = first + b
                            for c in range(2):
                                dve.wait_ge(S.row_cp[c], g + 2)
                                dve.wait_ge(S.e[c], g + 1)
                                f2 = [arena[:, p, ds(b * (2 * ROW) + (c * ROW + l.sums + h), 1)]
                                      for h in range(H)]
                                for h in range(H):
                                    ins = nc.vector.tensor_scalar(low[c][:, h, :], abB[p][:, 1, h, :], f2[h], SLOPE,
                                                                  ALU.add, ALU.mult)
                                ins.then_inc(S.low[c], 1)
                                dve.wait_ge(S.low[c], g + 2)
                                for h in range(H):
                                    ins = nc.vector.scalar_tensor_tensor(score[c][:, h, :], abB[p][:, 0, h, :], f2[h],
                                                                         low[c][:, h, :], ALU.add, ALU.max)
                                ins.then_inc(S.t[c], 1)
                    else:
                        par = load(dve, pbase, t + 2, 1, T * MAXB)
                        dve.wait_ge(S.mask_in[p], par * 16 + 1)
                        apart(dve, S)
                        with dve.Fori(0, count) as b:
                            g = first + b
                            for c in range(2):
                                dve.wait_ge(S.pv[c], g + 1)
                                m = masks[p][:, ds(b, 1), c * P:(c + 1) * P].rearrange("q a w -> q (a w)")
                                nc.vector.tensor_scalar(mask32[c][:, :], m, -1.0, None, ALU.is_gt).then_inc(S.e[c], 1)

                YD = (2, 2, 2, 1)[l.index]

                def finish(t, p, i):
                    k = [0]

                    def step(ins):
                        k[0] += 1
                        ins.then_inc(S.yd, 1)
                        dve.wait_ge(S.yd, t * YD + k[0] + 1)

                    dve.wait_ge(S.acc_done[p], i + 2)
                    x = own[p][:, 0:D]
                    xn = xo[p][:, 0:D]
                    dve.wait_ge(S.st_own[p], i * 16 + 1)
                    if l.att:
                        F = D // H
                        a = acc[p][:, 0:l.sums].rearrange("p (h f) -> p h f", h=H)
                        step(nc.vector.reciprocal(den[:, 0:H], a[:, :, F]))
                        yh = y[:, :].rearrange("p (h f) -> p h f", h=H)
                        ins = nc.vector.tensor_tensor(yh, a[:, :, 0:F], den[:, 0:H].unsqueeze(2).to_broadcast([P, H, F]),
                                                      ALU.mult)
                        ins.then_inc(S.acc_free[p], 1)
                        dve.wait_ge(S.acc_free[p], i + 2)
                        if l.index == 3:
                            nc.vector.tensor_tensor(xn, y[:, :], x, ALU.add).then_inc(S.xo[p], 1)
                        else:
                            nc.vector.tensor_scalar(yneg[:, :], y[:, :], 0.0, None, ALU.min).then_inc(S.y, 1)
                            dve.wait_ge(S.ye, t + 2)
                            step(nc.vector.scalar_tensor_tensor(y[:, :], y[:, :], 0.0, yneg[:, :], ALU.max, ALU.add))
                            nc.vector.scalar_tensor_tensor(xn, y[:, :], -1.0, x, ALU.add, ALU.add)\
                              .then_inc(S.xo[p], 1)
                    else:
                        step(nc.vector.tensor_scalar(den[:, 0:1], acc[p][:, D:D + 1], 1.0, None, ALU.max))
                        step(nc.vector.reciprocal(den[:, 1:2], den[:, 0:1]))
                        dve.wait_ge(S.own_in[p], 16 * (i + 1) + 1)
                        nc.vector.scalar_tensor_tensor(y[:, :], acc[p][:, 0:D], den[:, 1:2], own[p][:, D:2 * D],
                                                       ALU.mult, ALU.add).then_inc(S.acc_free[p], 1)
                        dve.wait_ge(S.acc_free[p], i + 2)
                        nc.vector.scalar_tensor_tensor(xn, y[:, :], 0.0, x, ALU.max, ALU.add)\
                          .then_inc(S.xo[p], 1)
                    assert k[0] == YD
                    if nxt:
                        dve.wait_ge(S.xo[p], i + 2)
                        norm(dve, S, nxt, t, p, i)

                def main(t, p, i):
                    scores(t, p, i)
                    finish(t, p, i)

                tiles(dve, maxima, main)

        def phase(name, program, Sems):
            S = Sems(nc, name)
            for s in S.all:
                if s not in S.by_pool:
                    nc.gpsimd.sem_inc(s, 1)
            nc.all_engine_barrier()
            with nc.Block() as blk:
                program(blk, S)
            nc.clear_and_free_semaphores(S.all)
            nc.all_engine_barrier()

        phase("list_", listing, ListingSems)
        for l in LAYERS:
            nxt = LAYERS[l.index + 1] if l.index < 3 else None
            phase(f"layer{l.index}_", lambda blk, S, l=l, nxt=nxt: layer(blk, l, nxt, S), LayerSems)


_INS = ['x', 'adj', 'L0_gnn_W', 'L0_gnn_a', 'L1_gnn_W_self', 'L1_gnn_b_self', 'L1_gnn_W_nb', 'L1_gnn_b_nb',
        'L1_gnn_W_comb', 'L1_gnn_b_comb', 'L2_gnn_W_w', 'L2_gnn_W_b', 'L2_gnn_a', 'L3_gnn_W', 'L3_gnn_a1', 'L3_gnn_a2']


def kernel(**inputs):
    import numpy as _np
    import concourse.bacc as _bacc
    from concourse import mybir as _mybir
    from concourse.bass_utils import run_bass_kernel_spmd as _run

    nc = _bacc.Bacc("TRN2", target_bir_lowering=False, num_devices=1)
    arrays, aps = {}, {}
    for name in _INS:
        a = _np.ascontiguousarray(inputs[name])
        arrays[f"in_{name}_dram"] = a
        aps[name] = nc.dram_tensor(f"in_{name}_dram", a.shape, _mybir.dt.from_np(a.dtype), kind="ExternalInput").ap()
    out = nc.dram_tensor("out_0_dram", (4096, 256), _mybir.dt.float32, kind="ExternalOutput").ap()
    build(nc, aps, out)
    r = _run(nc, [arrays], core_ids=[0])
    return r.results[0]["out_0_dram"]
```

```python
from contextlib import ExitStack

import numpy as np
import concourse.bass as bass
from concourse import mybir

ALU = mybir.AluOpType
ACT = mybir.ActivationFunctionType
AX = mybir.AxisListType
F32, BF16 = mybir.dt.float32, mybir.dt.bfloat16
I32, I16, U32 = mybir.dt.int32, mybir.dt.int16, mybir.dt.uint32
ds = bass.ds

P = 128
N = 4096
D = 256
T = N // P
JB = N // P
KC = D // P
W = 2 * P
MAXB = N // W
BIG = 1e30
FLOOR = -1e20
SLOPE = 0.2
EPS = 1e-5


class Layer:

    def __init__(self, index, heads, bias):
        self.index, self.heads, self.bias = index, heads, bias
        self.att = heads > 0
        self.own = 0 if heads else D
        self.sums = heads * (D // heads + 1) if heads else D + 1
        self.row = self.sums + heads
        self.cols = 2 * D if not heads else D + 2 * heads


LAYERS = [Layer(0, 1, False), Layer(1, 0, True), Layer(2, 8, True), Layer(3, 1, False)]
ROW = max(l.row for l in LAYERS)
OWN = D + max(l.own for l in LAYERS)

class Sems:

    def __init__(self, nc, name):
        self.nc, self.name, self.all = nc, name, []
        self.apart = self.one("apart")
        self.vln = self.one("vln")
        self.rstd = self.one("rstd")
        self.hc = self.one("hc")
        self.hT_ps = self.one("hT_ps")
        self.hT = self.one("hT")
        self.o_ps = self.one("o_ps")
        self.o = self.one("o")
        self.hs = self.one("hs")
        self.st_tab = self.two("st_tab")
        self.st_own = self.two("st_own")
        self.xo = self.two("xo")

    def one(self, what):
        self.all.append(self.nc.alloc_semaphore(name=self.name + what))
        return self.all[-1]

    def two(self, what):
        return [self.one(f"{what}{p}") for p in range(2)]


class ListingSems(Sems):
    def __init__(self, nc, name):
        super().__init__(nc, name)
        self.const = self.one("const")
        self.ident = self.one("ident")
        self.w_in = self.one("w_in")
        self.ini = self.one("ini")
        self.wt = self.one("wt")
        self.wtc = self.one("wtc")
        self.wprod = self.one("wprod")
        self.wset = self.one("wset")
        self.v = self.one("v")
        self.flag = self.one("flag")
        self.pre = self.one("pre")
        self.rankv = self.one("rankv")
        self.base = self.one("base")
        self.mt = self.one("mt")
        self.mtc = self.one("mtc")
        self.done = self.one("done")
        self.col = self.one("col")
        self.blk_out = self.one("blk_out")
        self.cnt = self.two("cnt")
        self.onehot = self.two("onehot")
        self.picked = self.two("picked")
        self.blk = self.two("blk")
        self.indexed = self.two("indexed")
        self.x_in = self.two("x_in")
        self.x_used = self.two("x_used")
        self.mask_in = self.two("mask_in")
        self.by_pool = self.mask_in


class LayerSems(Sems):
    def __init__(self, nc, name):
        super().__init__(nc, name)
        self.yd = self.one("yd")
        self.tabs = self.one("tabs")
        self.cs_ps = self.one("cs_ps")
        self.cs = self.one("cs")
        self.mx = self.one("mx")
        self.abps = self.one("abps")
        self.ab_cp = self.one("ab_cp")
        self.y = self.one("y")
        self.ye = self.one("ye")
        self.own_in = self.two("own_in")
        self.maskf_in = self.one("maskf_in")
        self.masks_in = self.one("masks_in")
        self.acc_done = self.two("acc_done")
        self.acc_free = self.two("acc_free")
        self.idx = self.two("idx")
        self.row_cp = self.two("row_cp")
        self.z = self.two("z")
        self.zx = self.two("zx")
        self.ab = self.two("ab")
        self.low = self.two("low")
        self.t = self.two("t")
        self.nm = self.two("nm")
        self.e = self.two("e")
        self.pv = self.two("pv")
        self.row_in = self.two("row_in")
        self.by_pool = self.row_in


def build(nc, A, out):
    with ExitStack() as ctx:
        def sb(name, shape, dt=F32):
            return ctx.enter_context(nc.sbuf_tensor(name, shape, dt))

        table = [nc.dram_tensor(f"table{l.index}", [N, l.row], F32, kind="Internal").ap() for l in LAYERS]
        own_d = [A["x"]] + [nc.dram_tensor(f"own{l.index}", [N, D + l.own], F32, kind="Internal").ap()
                            for l in LAYERS[1:]]
        block_d = nc.dram_tensor("block_masks", [(T + 1) * MAXB * P, W], BF16, kind="Internal").ap()

        identf = sb("identf", [P, P])
        identb = sb("identb", [P, 4, P], BF16)
        onesf = sb("onesf", [P, P])
        upper = sb("upper", [P, P], BF16)
        onesb = sb("onesb", [P, P], BF16)
        zrow = sb("zrow", [1, 512], BF16)
        wp = [sb(f"wp{l.index}", [P, KC, l.cols]) for l in LAYERS]
        brow = [sb(f"brow{l.index}", [1, l.cols]) if l.bias else None for l in LAYERS]
        raw = [sb(f"raw{i}", [P, KC, D]) for i in range(4)]
        rawT = [sb(f"rawT{i}", [P, KC, D]) for i in range(2)]
        comb = sb("comb", [P, 2 * KC, D])
        bcol = sb("bcol", [P, 2, KC])
        bcomb = sb("bcomb", [1, D])
        avec = [sb("avec0", [P, 2, D]), None, sb("avec2", [P, 2, 32]), sb("avec3", [P, 2, D])]
        prod = sb("prod", [P, D])
        index = sb("index", [P, 2 * (T + 1) * MAXB], I32)
        base = sb("base", [1, T + 2], I32)
        blocks = sb("blocks", [1, T], I32)
        nblkf = sb("nblkf", [1, 1])
        nblk = sb("nblk", [1, 4], I32)
        arena = sb("arena", [P, 2, MAXB * 2 * ROW])
        flat = arena[:, :, :].rearrange("p a b -> p (a b)")
        at = [0]

        def carve(words, dt, pattern=None, **k):
            v = flat[:, at[0]:at[0] + words].bitcast(dt)
            at[0] += words
            return v.rearrange(pattern, **k) if pattern else v

        MT = P + 2
        maskN = [carve(N // 2, BF16) for _ in range(2)]
        maskT = [carve(JB * MT // 2, BF16, "p (b m) -> p b m", b=JB) for _ in range(2)]
        onehot = [carve(N // 2, BF16, "p (k b) -> p k b", b=JB) for _ in range(2)]
        slots = carve(N // 2, I16, "p (k b) -> p k b", b=JB)
        assert at[0] <= 2 * MAXB * 2 * ROW
        flag = sb("flag", [P, JB], BF16)
        cum = sb("cum", [P, JB])
        rank = sb("rank", [P, JB])
        rank16 = sb("rank16", [P, 2, JB], I16)
        place32 = sb("place32", [P, JB, 2], I32)
        block = [sb(f"block{c}", [P, P], BF16) for c in range(2)]
        own = [sb(f"own_{p}", [P, OWN]) for p in range(2)]
        xo = [sb(f"xo_{p}", [P, OWN]) for p in range(2)]
        tab = [sb(f"tab_{p}", [P, ROW]) for p in range(2)]
        maskf = sb("maskf", [P, MAXB, W], BF16)
        masks = sb("masks", [P, MAXB, W], BF16)
        rowsc = [sb(f"rowsc{k}", [P, T * 8]) for k in range(2)]
        rows = [sb(f"rows_{c}", [P, ROW]) for c in range(2)]
        idx = [sb(f"idx_{c}", [P, 1], I32) for c in range(2)]
        scmax = [sb(f"scmax_{p}", [P, 8, 2 * MAXB]) for p in range(2)]
        small = sb("small", [P, 6, 8])
        ab = [sb(f"ab_{p}", [P, 2, 8]) for p in range(2)]
        none = [sb(f"none_{p}", [P, P]) for p in range(2)]
        abB = [sb(f"abB_{p}", [P, 2, 8, P]) for p in range(2)]
        low = [sb(f"low_{c}", [P, 8, P]) for c in range(2)]
        score = [sb(f"score_{c}", [P, 8, P]) for c in range(2)]
        prob = [sb(f"prob_{c}", [P, 8, P]) for c in range(2)]
        mask32 = [sb(f"mask32_{c}", [P, P]) for c in range(2)]
        hsum = sb("hsum", [P, ROW])
        csum = sb("csum", [P, ROW])
        stats = sb("stats", [P, 6])
        mv = sb("mv", [P, 2])
        veps = sb("veps", [P, 1])
        mhalf = sb("mhalf", [P, 1])
        rstd = sb("rstd", [P, 1])
        hc = sb("hc", [P, D])
        hT = sb("hT", [P, KC, P])
        den = sb("den", [P, 8])
        y = sb("y", [P, D])
        yneg = sb("yneg", [P, D])
        bank = [ctx.enter_context(nc.psum_tensor(f"bank{i}", [P, 512], F32)) for i in range(8)]
        z = [bank[0:2], bank[2:4]]
        acc = bank[4:6]
        tpb, opb = bank[6], bank[7]
        tb16 = [bank[i][:, :].bitcast(BF16).rearrange("p (b i) -> p b i", b=8) for i in range(2)]
        counts, ranks, picked = bank[4], bank[5], bank[2:4]

        def tiles(eng, *steps):
            leads = [lead for _, lead in steps]

            def run(t):
                for step, lead in steps:
                    if 0 <= t + lead < T:
                        step(t + lead, (t + lead) % 2, (t + lead) // 2)

            lo = -min(leads + [0])
            lo += lo % 2
            hi = T - max(leads + [0])
            hi -= hi % 2
            for t in range(-max(leads), lo):
                run(t)
            with eng.Fori(0, (hi - lo) // 2) as j:
                for q in range(2):
                    for step, lead in steps:
                        c = lo + q + lead
                        step(j * 2 + c, c % 2, j + c // 2)
            for t in range(hi, T - min(leads)):
                run(t)

        def load(eng, tensor, at_, lo, hi):
            return eng.value_load(tensor[0:1, ds(at_, 1)], min_val=lo, max_val=hi)

        def apart(eng, S):
            eng.sem_inc(S.apart, 1)

        def blocks_of(eng, t):
            return load(eng, base, t, 0, T * MAXB - 1), load(eng, blocks, t, 1, MAXB)

        def rows_of(ap, t):
            return ap[ds(t * P, P), :]


        def stores(sp, S, l):
            def step(t, p, i):
                sp.wait_ge(S.o, t + 2)
                apart(sp, S)
                sp.dma_start(rows_of(table[l.index], t), tab[p][:, 0:l.row]).then_inc(S.st_tab[p], 16)
                if l.index:
                    sp.dma_start(rows_of(own_d[l.index], t), xo[p][:, 0:D + l.own]).then_inc(S.st_own[p], 16)
            return step

        def root(pool, S):
            def step(t, p, i):
                pool.wait_ge(S.vln, t * 3 + 3 + 1)
                nc.gpsimd.tensor_tensor(rstd[:, :], veps[:, :], mhalf[:, :], ALU.pow).then_inc(S.rstd, 1)
            return step

        def add_up(pool, S, l):
            def step(t, p, i):
                pool.wait_ge(S.o, t + 2)
                pool.wait_ge(S.hs, t + 2)
                nc.gpsimd.tensor_tensor(hsum[:, 0:l.sums], hsum[:, 0:l.sums], tab[p][:, 0:l.sums], ALU.add)\
                  .then_inc(S.hs, 1)
            return step

        def turn(pe, S):
            def step(t, p, i):
                pe.wait_ge(S.hc, t + 2)
                pe.wait_ge(S.hT, t + 1)
                for k in range(KC):
                    last = nc.tensor.transpose(tpb[:, k * P:(k + 1) * P], hc[:, k * P:(k + 1) * P], identf[:, :])
                last.then_inc(S.hT_ps, 1)
            return step

        def turn_out(act, S):
            def step(t, p, i):
                act.wait_ge(S.hT_ps, t + 2)
                act.wait_ge(S.o_ps, t + 1)
                nc.scalar.activation(hT[:, :, :].rearrange("p k i -> p (k i)"), tpb[:, 0:D], ACT.Relu)\
                  .then_inc(S.hT, 1)
            return step

        def project(pe, S, l):
            def step(t, p, i):
                pe.wait_ge(S.hT, t + 2)
                pe.wait_ge(S.o, t + 1)
                o = opb[:, 0:l.cols]
                for k in range(KC):
                    last = nc.tensor.matmul(o, hT[:, k, :], wp[l.index][:, k, :], start=(k == 0),
                                            stop=(k == KC - 1 and not l.bias))
                if l.bias:
                    last = nc.tensor.matmul(o, onesf[0:1, :], brow[l.index][:, :], start=False, stop=True)
                last.then_inc(S.o_ps, 1)
            return step

        def project_out(act, S, l):
            def step(t, p, i):
                H = l.heads
                act.wait_ge(S.o_ps, t + 2)
                act.wait_ge(S.st_tab[p], i * 16 + 1)
                if l.att:
                    F = D // H
                    dst = tab[p][:, 0:l.sums].rearrange("p (h f) -> p h f", h=H)[:, :, 0:F]
                    nc.scalar.copy(dst, opb[:, 0:D].rearrange("p (h f) -> p h f", h=H))
                    nc.scalar.copy(tab[p][:, l.sums:l.row], opb[:, D:D + H])
                    nc.scalar.copy(rowsc[l.index % 2][:, ds(t * H, H)], opb[:, D + H:D + 2 * H]).then_inc(S.o, 1)
                else:
                    act.wait_ge(S.st_own[p], i * 16 + 1)
                    nc.scalar.copy(tab[p][:, 0:D], opb[:, 0:D])
                    nc.scalar.copy(xo[p][:, D:2 * D], opb[:, D:2 * D]).then_inc(S.o, 1)
            return step

        def stats_of(dve, S):
            def step(t, p, i):
                nc.vector.bn_stats(stats[:, :], xo[p][:, 0:D]).then_inc(S.vln, 1)
                dve.wait_ge(S.vln, t * 3 + 2)
                apart(dve, S)
                nc.vector.bn_aggr(mv[:, :], stats[:, :]).then_inc(S.vln, 1)
                dve.wait_ge(S.vln, t * 3 + 2 + 1)
                nc.vector.tensor_scalar(veps[:, :], mv[:, 1:2], EPS, None, ALU.add).then_inc(S.vln, 1)
            return step

        def center(dve, S):
            def step(t, p, i):
                dve.wait_ge(S.rstd, t + 2)
                dve.wait_ge(S.hT_ps, t + 1)
                nc.vector.tensor_scalar(hc[:, :], xo[p][:, 0:D], mv[:, 0:1], rstd[:, 0:1], ALU.subtract, ALU.mult)\
                  .then_inc(S.hc, 1)
            return step

        def listing(blk, S):
            @blk.sync
            def _(sp):
                def w_in(dst, src):
                    sp.dma_start(dst, src).then_inc(S.w_in, 16)
                w_in(wp[0][:, :, 0:D], A["L0_gnn_W"].rearrange("(c p) n -> p c n", p=P))
                for i, n in enumerate(("L1_gnn_W_self", "L1_gnn_W_nb", "L2_gnn_W_w", "L3_gnn_W")):
                    w_in(raw[i][:, :, :], A[n].rearrange("(c p) n -> p c n", p=P))
                w_in(comb[:, :, :], A["L1_gnn_W_comb"].rearrange("(c p) n -> p c n", p=P))
                w_in(avec[0][:, :, :].rearrange("p a d -> p (a d)"),
                     A["L0_gnn_a"].rearrange("d a -> (a d)").partition_broadcast(P))
                w_in(avec[2][:, :, :].rearrange("p a d -> p (a d)"),
                     A["L2_gnn_a"].rearrange("d a -> (a d)").partition_broadcast(P))
                w_in(avec[3][:, 0, :], A["L3_gnn_a1"].partition_broadcast(P))
                w_in(avec[3][:, 1, :], A["L3_gnn_a2"].partition_broadcast(P))
                with nc.allow_non_contiguous_dma(reason="two short columns"):
                    w_in(bcol[:, 0, :], A["L1_gnn_b_self"].rearrange("(c p) -> p c", p=P))
                    w_in(bcol[:, 1, :], A["L1_gnn_b_nb"].rearrange("(c p) -> p c", p=P))
                w_in(bcomb[:, :], A["L1_gnn_b_comb"].rearrange("(a d) -> a d", a=1))
                w_in(brow[2][:, 0:D], A["L2_gnn_W_b"].rearrange("(a d) -> a d", a=1))

                def x_tile(t, p, i):
                    sp.wait_ge(S.x_used[p], i + 1)
                    sp.dma_start(xo[p][:, 0:D], rows_of(A["x"], t)).then_inc(S.x_in[p], 16)

                def masks_out(t, p, i):
                    sp.wait_ge(S.base, t + 2)
                    first, count = blocks_of(sp, t)
                    with sp.Fori(0, count) as b:
                        g = first + b
                        for c in range(2):
                            sp.wait_ge(S.blk[c], g + 2)
                        for c in range(2):
                            sp.dma_start(block_d[ds(g * P, P), c * P:(c + 1) * P], block[c][:, :])\
                              .then_inc(S.blk_out, 16)

                tiles(sp, (x_tile, 0), (stores(sp, S, LAYERS[0]), -2), (masks_out, 0))
                total = load(sp, base, T, 1, T * MAXB)
                sp.wait_ge(S.blk_out, total * 32 + 1)
                apart(sp, S)
                for p in range(2):
                    sp.wait_ge(S.st_tab[p], 16 * T // 2 + 1)

            @blk.gpsimd
            def _(pool):
                nc.gpsimd.memset(identf[:, :], 0.0).then_inc(S.const, 1)
                nc.gpsimd.memset(upper[:, :], 1.0).then_inc(S.const, 1)
                nc.gpsimd.iota(slots, [[1, P], [0, JB]], base=0, channel_multiplier=0).then_inc(S.ident, 1)
                nc.gpsimd.iota(place32[:, :, 0], [[1, JB]], base=0, channel_multiplier=0).then_inc(S.ident, 1)
                nc.gpsimd.iota(place32[:, :, 1], [[0, JB]], base=0, channel_multiplier=1).then_inc(S.ident, 1)
                pool.wait_ge(S.const, 2 + 1)
                nc.gpsimd.affine_select(out=identf[:, :], in_=identf[:, :], compare_op=ALU.not_equal, fill=1.0,
                                        base=0, pattern=[[-1, P]], channel_multiplier=1).then_inc(S.ident, 1)
                nc.gpsimd.affine_select(out=upper[:, :], in_=upper[:, :], compare_op=ALU.is_ge, fill=0.0,
                                        base=0, pattern=[[1, P]], channel_multiplier=-1).then_inc(S.ident, 1)
                nc.gpsimd.memset(hsum[:, :], 0.0).then_inc(S.hs, 1)

                def adjacency(t, p, i):
                    pool.wait_ge(S.cnt[p], i + 1)
                    pool.dma_start(maskN[p], rows_of(A["adj"], t)).then_inc(S.mask_in[p], 16)

                tiles(pool, (adjacency, 2), (root(pool, S), -1), (add_up(pool, S, LAYERS[0]), -2))
                pool.wait_ge(S.base, T + 1)


            @blk.tensor
            def _(pe):
                pe.wait_ge(S.ident, 5 + 1)
                pe.wait_ge(S.w_in, 16 * 14 + 1)
                for i in range(4):
                    for cc in range(KC):
                        for rc in range(KC):
                            k = cc * KC + rc
                            last = nc.tensor.transpose(bank[i][:, k * P:(k + 1) * P],
                                                       raw[i][:, rc, cc * P:(cc + 1) * P], identf[:, :])
                    last.then_inc(S.wt, 1)
                pe.wait_ge(S.wtc, 2 + 1)
                for which, off in ((1, KC), (0, 0)):
                    for kc in range(KC):
                        o = bank[4 + which][:, kc * D:(kc + 1) * D]
                        for mc in range(KC):
                            last = nc.tensor.matmul(o, rawT[which][:, mc, kc * P:(kc + 1) * P], comb[:, off + mc, :],
                                                    start=(mc == 0), stop=(mc == KC - 1))
                    last.then_inc(S.wprod, 1)
                pe.wait_ge(S.ini, 2 + 1)
                for s in range(2):
                    for mc in range(KC):
                        nc.tensor.matmul(bank[6][0:1, 0:D], bcol[:, s, mc:mc + 1], comb[:, KC * s + mc, :],
                                         start=(s == 0 and mc == 0), stop=False)
                nc.tensor.matmul(bank[6][0:1, 0:D], onesf[0:1, 0:1], bcomb[:, :], start=False, stop=True)\
                  .then_inc(S.wprod, 1)
                pe.wait_ge(S.wset, 1 + 1)

                def transposes(t, p, i):
                    pe.wait_ge(S.mask_in[p], 16 * (i + 1))
                    for q in range(4):
                        pe.wait_ge(S.mtc, t * 4 + max(q - 1, 0) + 1)
                        for b in range(8):
                            jb = 8 * q + b
                            last = nc.tensor.transpose(tb16[q % 2][:, b, :], maskN[p][:, jb * P:(jb + 1) * P],
                                                       identb[:, 0, :])
                        last.then_inc(S.mt, 1)
                    pe.wait_ge(S.flag, t + 1)
                    for jb in range(JB):
                        last = nc.tensor.matmul(counts[:, jb:jb + 1], maskN[p][:, jb * P:(jb + 1) * P],
                                                onesb[:, 0:1], start=True, stop=True)
                    last.then_inc(S.cnt[p], 1)

                def ranks_of(t, p, i):
                    pe.wait_ge(S.flag, t + 2)
                    pe.wait_ge(S.base, t + 1)
                    nc.tensor.matmul(ranks[:, 0:JB], upper[:, :], flag[:, :], start=True, stop=True)
                    nc.tensor.matmul(ranks[:, JB:2 * JB], onesb[:, :], flag[:, :], start=True, stop=True)\
                      .then_inc(S.pre, 1)

                def pick(t, p, i):
                    pe.wait_ge(S.base, t + 2)
                    first, count = blocks_of(pe, t)
                    pe.wait_ge(S.mtc, t * 4 + 4 + 1)
                    apart(pe, S)
                    with pe.Fori(0, count) as b:
                        g = first + b
                        for c in range(2):
                            pe.wait_ge(S.onehot[c], g + 2)
                            pe.wait_ge(S.blk[c], g + 1)
                            pe.wait_ge(S.indexed[c], g + 1)
                            for jb in range(JB):
                                mm = nc.tensor.matmul(picked[c][:, 0:MT], onehot[c][:, :, jb], maskT[p][:, jb, :],
                                                      start=(jb == 0), stop=(jb == JB - 1))
                            mm.then_inc(S.picked[c], 1)

                tiles(pe, (transposes, 1), (project(pe, S, LAYERS[0]), -2), (ranks_of, 1), (pick, 0),
                      (turn(pe, S), -1))


            @blk.scalar
            def _(act):
                act.wait_ge(S.wset, 1 + 1)

                def keep_masks(t, p, i):
                    for q in range(4):
                        act.wait_ge(S.mt, t * 4 + q + 2)
                        nc.scalar.copy(maskT[p][:, 8 * q:8 * q + 8, 0:P], tb16[q % 2]).then_inc(S.mtc, 1)

                def block_masks(t, p, i):
                    act.wait_ge(S.base, t + 2)
                    first, count = blocks_of(act, t)
                    with act.Fori(0, count) as b:
                        g = first + b
                        act.wait_ge(S.blk_out, g * 32 + 1)
                        for c in range(2):
                            act.wait_ge(S.picked[c], g + 2)
                            nc.scalar.activation(block[c][:, :], picked[c][:, 0:P], ACT.Copy, scale=BIG, bias=-BIG)\
                              .then_inc(S.blk[c], 1)

                tiles(act, (keep_masks, 1), (project_out(act, S, LAYERS[0]), -2), (block_masks, 0),
                      (turn_out(act, S), -1))


            @blk.vector
            def _(dve):
                V = [0]

                def link(ins):
                    V[0] += 1
                    ins.then_inc(S.v, 1)
                    dve.wait_ge(S.v, V[0] + 1)

                nc.vector.memset(onesf[:, :], 1.0).then_inc(S.ini, 1)
                nc.vector.memset(mhalf[:, :], -0.5)
                nc.vector.memset(zrow[:, :], 0.0)
                nc.vector.memset(base[:, :], 0)
                nc.vector.memset(index[:, :], 0)
                for p in range(2):
                    nc.vector.memset(tab[p][:, :], 1.0)
                nc.vector.memset(brow[1][:, 0:D], 0.0)
                link(nc.vector.memset(onesb[:, :], 1.0))
                nc.vector.memset(none[0][:, :], 0.0).then_inc(S.ini, 1)
                dve.wait_ge(S.ident, 5 + 1)
                link(nc.vector.tensor_copy(identb[:, :, :], identf[:, :].unsqueeze(1).to_broadcast([P, 4, P])))
                for p in range(2):
                    link(nc.vector.tensor_copy(maskT[p][:, :, P:P + 2], place32[:, :, :]))
                for i, dst in enumerate((rawT[0][:, :, :], rawT[1][:, :, :], wp[2][:, :, 0:D], wp[3][:, :, 0:D])):
                    dve.wait_ge(S.wt, i + 2)
                    ins = nc.vector.tensor_copy(dst, bank[i][:, :].rearrange("p (k n) -> p k n", k=KC))
                    if i < 2:
                        ins.then_inc(S.wtc, 1)
                    else:
                        link(ins)
                for n, which in enumerate((1, 0)):
                    dve.wait_ge(S.wprod, n + 2)
                    link(nc.vector.tensor_copy(wp[1][:, :, n * D:(n + 1) * D],
                                               bank[4 + which][:, :].rearrange("p (k n) -> p k n", k=KC)))
                dve.wait_ge(S.wprod, 3 + 1)
                link(nc.vector.tensor_copy(brow[1][:, D:2 * D], bank[6][0:1, 0:D]))
                dve.wait_ge(S.w_in, 16 * 14 + 1)
                for l in (LAYERS[0], LAYERS[2], LAYERS[3]):
                    H, F = l.heads, D // l.heads
                    srcs = [wp[l.index][:, k, :] for k in range(KC)] + ([brow[2][:, :]] if l.bias else [])
                    for w in srcs:
                        n = w.shape[0]
                        for s in range(2):
                            pv = prod[0:n, :].rearrange("p (h f) -> p h f", h=H)
                            av = avec[l.index][0:n, 1 - s, :].unsqueeze(1).to_broadcast([n, H, F])
                            link(nc.vector.tensor_tensor(pv, w[:, 0:D].rearrange("p (h f) -> p h f", h=H), av, ALU.mult))
                            link(nc.vector.tensor_reduce(w[:, D + s * H:D + s * H + H], pv, AX.X, ALU.add))
                nc.vector.memset(scmax[0][:, :, :], -BIG).then_inc(S.wset, 1)

                R = 7

                def flags(t, p, i):
                    dve.wait_ge(S.cnt[p], i + 2)
                    dve.wait_ge(S.pre, t + 1)
                    nc.vector.tensor_scalar(flag[:, :], counts[:, 0:JB], 0.0, None, ALU.is_gt).then_inc(S.flag, 1)

                def ranking(t, p, i):
                    dve.wait_ge(S.pre, t + 2)
                    k = [0]

                    def step(ins):
                        k[0] += 1
                        ins.then_inc(S.rankv, 1)
                        dve.wait_ge(S.rankv, t * R + k[0] + 1)

                    tot = ranks[:, JB:2 * JB]
                    step(nc.vector.tensor_tensor_scan(cum[:, :], onesf[:, 0:JB], tot, 0.0, ALU.mult, ALU.add))
                    step(nc.vector.tensor_scalar(nblk[:, 0:1], cum[0:1, JB - 1:JB], float(W - 1), None, ALU.add))
                    step(nc.vector.tensor_scalar(nblk[:, 1:2], nblk[:, 0:1], 8, None, ALU.arith_shift_right))
                    step(nc.vector.tensor_scalar(nblkf[:, :], nblk[:, 1:2], 1.0, None, ALU.max))
                    nc.vector.tensor_copy(blocks[:, ds(t, 1)], nblkf[:, :])
                    nc.vector.tensor_tensor(base[:, ds(t + 1, 1)], base[:, ds(t, 1)], nblkf[:, :], ALU.add)
                    step(nc.vector.scalar_tensor_tensor(rank[:, :], ranks[:, 0:JB], 2.0 * N - 1, cum[:, :],
                                                        ALU.add, ALU.add))
                    step(nc.vector.tensor_tensor(rank[:, :], rank[:, :], tot, ALU.subtract))
                    step(nc.vector.tensor_tensor(rank[:, :], rank[:, :], flag[:, :], ALU.mult))
                    assert k[0] == R
                    for c in range(2):
                        ins = nc.vector.tensor_scalar(rank16[:, c, :], rank[:, :], -2.0 * N - c * P, None, ALU.add)
                    ins.then_inc(S.base, 1)

                def columns(t, p, i):
                    dve.wait_ge(S.base, t + 2)
                    apart(dve, S)
                    first, count = blocks_of(dve, t)
                    with dve.Fori(0, count) as b:
                        g = first + b
                        for c in range(2):
                            dve.wait_ge(S.picked[c], g + 1)
                            dve.wait_ge(S.done, g * 2 + 1)
                            nc.vector.tensor_tensor(onehot[c], slots,
                                                    rank16[:, c, :].unsqueeze(1).to_broadcast([P, P, JB]),
                                                    ALU.is_equal).then_inc(S.onehot[c], 1)
                        for c in range(2):
                            dve.wait_ge(S.onehot[c], g + 2)
                            nc.vector.tensor_scalar(rank16[:, c, :], rank16[:, c, :], float(W), None, ALU.subtract)\
                              .then_inc(S.done, 1)
                        for c in range(2):
                            dve.wait_ge(S.picked[c], g + 2)
                            dve.wait_ge(S.blk[c], g + 2)
                            nc.vector.tensor_scalar(rank[:, c:c + 1], picked[c][:, P:P + 1], float(P), None, ALU.mult)\
                              .then_inc(S.col, 1)
                            dve.wait_ge(S.col, g * 2 + c + 2)
                            nc.vector.tensor_tensor(index[:, ds(g * 2 + c, 1)], rank[:, c:c + 1],
                                                    picked[c][:, P + 1:P + 2], ALU.add).then_inc(S.indexed[c], 1)

                def x_stats(t, p, i):
                    dve.wait_ge(S.x_in[p], 16 * (i + 1) + 1)
                    stats_of(dve, S)(t, p, i)

                def x_center(t, p, i):
                    center(dve, S)(t, p, i)
                    dve.wait_ge(S.hc, t + 2)
                    dve.sem_inc(S.x_used[p], 1)

                tiles(dve, (flags, 1), (x_stats, -1), (columns, 0), (ranking, 1), (x_center, -1))

        def layer(blk, l, nxt, S):
            @blk.sync
            def _(sp):
                def masks_in(t, into, sem):
                    first, count = blocks_of(sp, t)
                    with sp.Fori(0, count) as b:
                        g = first + b
                        sp.dma_start(into[:, ds(b, 1), :].rearrange("q a w -> q (a w)"),
                                     block_d[ds(g * P, P), :]).then_inc(sem, 16)

                def for_maxima(t, p, i):
                    if l.att:
                        before = load(sp, base, t, 0, T * MAXB)
                        for c in range(2):
                            sp.wait_ge(S.z[c], before + 1)
                            apart(sp, S)
                        masks_in(t, maskf, S.maskf_in)

                def for_scores(t, p, i):
                    before = load(sp, base, t, 0, T * MAXB)
                    for c in range(2):
                        sp.wait_ge(S.nm[c] if l.att else S.e[c], before + 1)
                        apart(sp, S)
                    masks_in(t, masks, S.masks_in)

                def own_in(t, p, i):
                    sp.wait_ge(S.xo[p], i + 1)
                    apart(sp, S)
                    sp.dma_start(own[p][:, 0:D + l.own], rows_of(own_d[l.index], t)).then_inc(S.own_in[p], 16)

                def result_out(t, p, i):
                    sp.wait_ge(S.xo[p], i + 2)
                    apart(sp, S)
                    sp.dma_start(rows_of(out, t), xo[p][:, 0:D]).then_inc(S.st_own[p], 16)

                if nxt:
                    tiles(sp, (for_maxima, 2), (stores(sp, S, nxt), -2), (own_in, 1), (for_scores, 1))
                else:
                    tiles(sp, (for_maxima, 2), (own_in, 1), (result_out, -1), (for_scores, 1))
                for p in range(2):
                    if nxt:
                        sp.wait_ge(S.st_tab[p], 16 * T // 2 + 1)
                    sp.wait_ge(S.st_own[p], 16 * T // 2 + 1)

            @blk.gpsimd
            def _(pool):
                if nxt and nxt.att:
                    if l.att:
                        pool.wait_ge(S.cs_ps, 1 + 1)
                    nc.gpsimd.memset(hsum[:, :], 0.0).then_inc(S.hs, 1)

                def gather(c):
                    nc.gpsimd.indirect_dma_start(
                        rows[c][:, 0:l.row], None, table[l.index][:, :],
                        bass.IndirectOffsetOnAxis(idx[c][:, :].bitcast(U32), 0)).then_inc(S.row_in[c], 16)

                for c in range(2):
                    nc.gpsimd.tensor_copy(idx[c][:, :], index[:, c:c + 1]).then_inc(S.idx[c], 1)
                for c in range(2):
                    pool.wait_ge(S.idx[c], 1 + 1)
                    gather(c)

                def next_rows(t, p, i):
                    first, count = blocks_of(pool, t)
                    with pool.Fori(0, count) as b:
                        g = first + b
                        for c in range(2):
                            pool.wait_ge(S.row_cp[c], g + 2)
                            nc.gpsimd.tensor_copy(idx[c][:, :], index[:, ds(g * 2 + 2 + c, 1)]).then_inc(S.idx[c], 1)
                        for c in range(2):
                            pool.wait_ge(S.idx[c], g + 3)
                            if l.att:
                                pool.wait_ge(S.z[c], g + 2)
                            apart(pool, S)
                            gather(c)

                def mask_add(t, p, i):
                    if not l.att:
                        return
                    first, count = blocks_of(pool, t)
                    pool.wait_ge(S.masks_in, (first + count) * 16 + 1)
                    apart(pool, S)
                    with pool.Fori(0, count) as b:
                        g = first + b
                        for c in range(2):
                            pool.wait_ge(S.t[c], g + 2)
                            sc = score[c][:, 0:l.heads, :]
                            m = masks[:, ds(b, 1), c * P:(c + 1) * P]
                            nc.gpsimd.tensor_tensor(sc, sc, m.to_broadcast([P, l.heads, P]), ALU.add)\
                              .then_inc(S.nm[c], 1)

                steps = [(next_rows, 1)]
                if nxt:
                    steps.append((root(pool, S), -1))
                steps.append((mask_add, 0))
                if nxt and nxt.att:
                    steps.append((add_up(pool, S, nxt), -2))
                tiles(pool, *steps)
                total = load(pool, base, T, 1, T * MAXB)
                for c in range(2):
                    pool.wait_ge(S.row_in[c], total * 16 + 16)
                    apart(pool, S)

            @blk.tensor
            def _(pe):
                H = l.heads
                if l.att:
                    nc.tensor.matmul(opb[:, 0:l.sums], onesf[:, :], hsum[:, 0:l.sums], start=True, stop=True)\
                      .then_inc(S.cs_ps, 1)
                    pe.wait_ge(S.cs, 1 + 1)

                def spread(t, p, i):
                    first, count = blocks_of(pe, t)
                    pe.wait_ge(S.maskf_in, (first + count) * 16 + 1)
                    pe.wait_ge(S.ab_cp, t + 1)
                    apart(pe, S)
                    hb = min(H, 4)
                    with pe.Fori(0, count) as b:
                        g = first + b
                        for c in range(2):
                            pe.wait_ge(S.row_in[c], g * 16 + 16)
                            pe.wait_ge(S.zx[c], g + 1)
                            m = maskf[:, ds(b, 1), c * P:(c + 1) * P].rearrange("q a w -> q (a w)")
                            for h in range(0, H, 4):
                                o = z[c][h // 4]
                                nc.tensor.matmul(o[:, 0:hb * P], m,
                                                 identb[:, 0:hb, :].rearrange("p a b -> p (a b)"),
                                                 start=True, stop=False)
                                for k in range(hb):
                                    s = l.sums + h + k
                                    last_mm = nc.tensor.matmul(
                                        o[:, k * P:(k + 1) * P], rows[c][:, s:s + 1].to_broadcast([P, P]),
                                        identf[:, :], start=False, stop=(k == hb - 1))
                            last_mm.then_inc(S.z[c], 1)

                def weigh(t, p, i):
                    first, count = blocks_of(pe, t)
                    a = acc[p]
                    F = D // H + 1 if H else l.row
                    pe.wait_ge(S.acc_free[p], i + 1)
                    nc.tensor.matmul(a[:, 0:l.sums], zrow[:, 0:P], zrow[:, 0:l.sums], start=True, stop=False)
                    with pe.Fori(0, count) as b:
                        g = first + b
                        for c in range(2):
                            pe.wait_ge(S.e[c], g + 2)
                            pe.wait_ge(S.row_cp[c], g + 2)
                            for h in range(max(H, 1)):
                                r = arena[:, p, ds(b * (2 * ROW) + (c * ROW + h * F), F)]
                                wt = prob[c][:, h, :] if l.att else mask32[c][:, :]
                                mm = nc.tensor.matmul(a[:, h * F:(h + 1) * F], wt, r, start=False, stop=False)
                            mm.then_inc(S.pv[c], 1)
                    if l.att:
                        nc.tensor.matmul(a[:, 0:l.sums], none[p][:, :], csum[:, 0:l.sums], start=False,
                                         stop=True).then_inc(S.acc_done[p], 1)
                    else:
                        nc.tensor.matmul(a[:, 0:l.sums], zrow[:, 0:P], zrow[:, 0:l.sums], start=False,
                                         stop=True).then_inc(S.acc_done[p], 1)

                def row_terms(t, p, i):
                    pe.wait_ge(S.ab[p], i + 2)
                    for v in range(2):
                        for h in range(H):
                            mm = nc.tensor.matmul(z[v][h // 4][:, (h % 4) * P:(h % 4 + 1) * P],
                                                  ab[p][:, v, h:h + 1].to_broadcast([P, P]), identf[:, :],
                                                  start=(h % 4 == 0), stop=(h % 4 == 3 or h == H - 1),
                                                  skip_group_check=True)
                    mm.then_inc(S.abps, 1)

                steps = [(spread, 1)] if l.att else []
                if nxt:
                    steps.append((project(pe, S, nxt), -2))
                if l.att:
                    steps.append((row_terms, 1))
                steps.append((weigh, 0))
                if nxt:
                    steps.append((turn(pe, S), -1))
                tiles(pe, *steps)

            @blk.scalar
            def _(act):
                H = l.heads
                if nxt:
                    act.wait_ge(S.tabs, 1 + 1)

                def keep(t, p, i):
                    first, count = blocks_of(act, t)
                    act.wait_ge(S.acc_done[p], i + 1)
                    apart(act, S)
                    with act.Fori(0, count) as b:
                        g = first + b
                        for c in range(2):
                            act.wait_ge(S.row_in[c], g * 16 + 16)
                            nc.scalar.copy(arena[:, p, ds(b * (2 * ROW) + c * ROW, l.row)],
                                           rows[c][:, 0:l.row]).then_inc(S.row_cp[c], 1)

                def weights(t, p, i):
                    first, count = blocks_of(act, t)
                    with act.Fori(0, count) as b:
                        g = first + b
                        for c in range(2):
                            act.wait_ge(S.nm[c], g + 2)
                            act.wait_ge(S.pv[c], g + 1)
                            nc.scalar.activation(prob[c][:, 0:H, :], score[c][:, 0:H, :], ACT.Exp)\
                              .then_inc(S.e[c], 1)

                def elu(t, p, i):
                    act.wait_ge(S.y, t + 2)
                    nc.scalar.activation(yneg[:, :], yneg[:, :], ACT.Exp).then_inc(S.ye, 1)

                def row_terms(t, p, i):
                    act.wait_ge(S.abps, t + 2)
                    for v in range(2):
                        for h in range(0, H, 4):
                            n = min(4, H)
                            mm = nc.scalar.copy(abB[p][:, v, h:h + n, :].rearrange("p h i -> p (h i)"),
                                                z[v][h // 4][:, 0:n * P])
                    mm.then_inc(S.ab_cp, 1)

                steps = [(keep, 1)]
                if nxt:
                    steps.append((project_out(act, S, nxt), -2))
                if l.index in (0, 2):
                    steps.append((elu, -1))
                if l.att:
                    steps += [(row_terms, 1), (weights, 0)]
                if nxt:
                    steps.append((turn_out(act, S), -1))
                tiles(act, *steps)

            @blk.vector
            def _(dve):
                H = l.heads
                for p in range(2):
                    ins = nc.vector.memset(tab[p][:, :], 1.0)
                ins.then_inc(S.tabs, 1)
                if l.att:
                    dve.wait_ge(S.cs_ps, 1 + 1)
                    nc.vector.tensor_copy(csum[:, 0:l.sums], opb[:, 0:l.sums]).then_inc(S.cs, 1)
                MX = 7

                def maxima(t, p, i):
                    first, count = blocks_of(dve, t)
                    k = [0]

                    def step(ins):
                        k[0] += 1
                        ins.then_inc(S.mx, 1)
                        dve.wait_ge(S.mx, t * MX + k[0] + 1)

                    step(nc.vector.memset(scmax[p][:, 0:H, :], -BIG))
                    apart(dve, S)
                    with dve.Fori(0, count) as b:
                        g = first + b
                        for c in range(2):
                            dve.wait_ge(S.z[c], g + 2)
                            for h in range(0, H, 4):
                                n = min(4, H)
                                ins = nc.vector.tensor_reduce(
                                    scmax[p][:, h:h + n, ds(b * 2 + c, 1)],
                                    z[c][h // 4][:, 0:n * P].rearrange("p (h i) -> p h i", h=n), AX.X, ALU.max)
                            ins.then_inc(S.zx[c], 1)
                    for c in range(2):
                        dve.wait_ge(S.zx[c], first + count + 1)
                    zm, s, m = small[:, 0, 0:H], small[:, 1, 0:H], small[:, 2, 0:H]
                    step(nc.vector.tensor_reduce(zm, scmax[p][:, 0:H, :], AX.X, ALU.max))
                    dve.wait_ge(S.abps, t + 1)
                    f1 = rowsc[l.index % 2][:, ds(t * H, H)]
                    step(nc.vector.tensor_tensor(s, f1, zm, ALU.add))
                    step(nc.vector.scalar_tensor_tensor(m, s, SLOPE, s, ALU.mult, ALU.max))
                    step(nc.vector.tensor_scalar(s, m, FLOOR, None, ALU.max))
                    nc.vector.tensor_tensor(ab[p][:, 0, 0:H], f1, s, ALU.subtract)
                    step(nc.vector.scalar_tensor_tensor(ab[p][:, 1, 0:H], s, -1.0 / SLOPE, f1, ALU.mult, ALU.add))
                    step(nc.vector.tensor_scalar(small[:, 3, 0:1], zm[:, 0:1], -0.1 * BIG, None, ALU.is_lt))
                    assert k[0] == MX
                    nc.vector.tensor_scalar(none[p][:, :], identf[:, :], small[:, 3, 0:1], None, ALU.mult)\
                      .then_inc(S.ab[p], 1)

                def scores(t, p, i):
                    first, count = blocks_of(dve, t)
                    if l.att:
                        dve.wait_ge(S.ab_cp, t + 2)
                        apart(dve, S)
                        with dve.Fori(0, count) as b:
                            g = first + b
                            for c in range(2):
                                dve.wait_ge(S.row_cp[c], g + 2)
                                dve.wait_ge(S.e[c], g + 1)
                                f2 = [arena[:, p, ds(b * (2 * ROW) + (c * ROW + l.sums + h), 1)]
                                      for h in range(H)]
                                for h in range(H):
                                    ins = nc.vector.tensor_scalar(low[c][:, h, :], abB[p][:, 1, h, :], f2[h], SLOPE,
                                                                  ALU.add, ALU.mult)
                                ins.then_inc(S.low[c], 1)
                                dve.wait_ge(S.low[c], g + 2)
                                for h in range(H):
                                    ins = nc.vector.scalar_tensor_tensor(score[c][:, h, :], abB[p][:, 0, h, :], f2[h],
                                                                         low[c][:, h, :], ALU.add, ALU.max)
                                ins.then_inc(S.t[c], 1)
                    else:
                        dve.wait_ge(S.masks_in, (first + count) * 16 + 1)
                        apart(dve, S)
                        with dve.Fori(0, count) as b:
                            g = first + b
                            for c in range(2):
                                dve.wait_ge(S.pv[c], g + 1)
                                m = masks[:, ds(b, 1), c * P:(c + 1) * P].rearrange("q a w -> q (a w)")
                                nc.vector.tensor_scalar(mask32[c][:, :], m, -1.0, None, ALU.is_gt).then_inc(S.e[c], 1)

                YD = (2, 2, 2, 1)[l.index]

                def link(ins, t, k):
                    ins.then_inc(S.yd, 1)
                    dve.wait_ge(S.yd, t * YD + k + 1)

                def divide(t, p, i):
                    dve.wait_ge(S.acc_done[p], i + 2)
                    if l.att:
                        F = D // H
                        a = acc[p][:, 0:l.sums].rearrange("p (h f) -> p h f", h=H)
                        link(nc.vector.reciprocal(den[:, 0:H], a[:, :, F]), t, 1)
                        yh = y[:, :].rearrange("p (h f) -> p h f", h=H)
                        ins = nc.vector.tensor_tensor(yh, a[:, :, 0:F], den[:, 0:H].unsqueeze(2).to_broadcast([P, H, F]),
                                                      ALU.mult)
                        ins.then_inc(S.acc_free[p], 1)
                        if l.index != 3:
                            dve.wait_ge(S.acc_free[p], i + 2)
                            nc.vector.tensor_scalar(yneg[:, :], y[:, :], 0.0, None, ALU.min).then_inc(S.y, 1)
                    else:
                        link(nc.vector.tensor_scalar(den[:, 0:1], acc[p][:, D:D + 1], 1.0, None, ALU.max), t, 1)
                        link(nc.vector.reciprocal(den[:, 1:2], den[:, 0:1]), t, 2)
                        dve.wait_ge(S.own_in[p], 16 * (i + 1) + 1)
                        nc.vector.scalar_tensor_tensor(y[:, :], acc[p][:, 0:D], den[:, 1:2], own[p][:, D:2 * D],
                                                       ALU.mult, ALU.add).then_inc(S.acc_free[p], 1)

                def result(t, p, i):
                    x = own[p][:, 0:D]
                    xn = xo[p][:, 0:D]
                    dve.wait_ge(S.own_in[p], 16 * (i + 1) + 1)
                    dve.wait_ge(S.st_own[p], i * 16 + 1)
                    dve.wait_ge(S.acc_free[p], i + 2)
                    if l.index == 3:
                        nc.vector.tensor_tensor(xn, y[:, :], x, ALU.add).then_inc(S.xo[p], 1)
                    elif l.index == 1:
                        nc.vector.scalar_tensor_tensor(xn, y[:, :], 0.0, x, ALU.max, ALU.add)\
                          .then_inc(S.xo[p], 1)
                    else:
                        dve.wait_ge(S.ye, t + 2)
                        link(nc.vector.scalar_tensor_tensor(y[:, :], y[:, :], 0.0, yneg[:, :], ALU.max, ALU.add), t, 2)
                        nc.vector.scalar_tensor_tensor(xn, y[:, :], -1.0, x, ALU.add, ALU.add)\
                          .then_inc(S.xo[p], 1)
                    if nxt:
                        dve.wait_ge(S.xo[p], i + 2)
                        stats_of(dve, S)(t, p, i)

                steps = [(divide, -1)]
                if l.att:
                    steps.append((maxima, 1))
                steps += [(result, -1), (scores, 0)]
                if nxt:
                    steps.append((center(dve, S), -1))
                tiles(dve, *steps)

        def phase(name, program, Sems):
            S = Sems(nc, name)
            for s in S.all:
                if s not in S.by_pool:
                    nc.gpsimd.sem_inc(s, 1)
            nc.all_engine_barrier()
            with nc.Block() as blk:
                program(blk, S)
            nc.clear_and_free_semaphores(S.all)
            nc.all_engine_barrier()

        phase("list_", listing, ListingSems)
        for l in LAYERS:
            nxt = LAYERS[l.index + 1] if l.index < 3 else None
            phase(f"layer{l.index}_", lambda blk, S, l=l, nxt=nxt: layer(blk, l, nxt, S), LayerSems)


_INS = ['x', 'adj', 'L0_gnn_W', 'L0_gnn_a', 'L1_gnn_W_self', 'L1_gnn_b_self', 'L1_gnn_W_nb', 'L1_gnn_b_nb',
        'L1_gnn_W_comb', 'L1_gnn_b_comb', 'L2_gnn_W_w', 'L2_gnn_W_b', 'L2_gnn_a', 'L3_gnn_W', 'L3_gnn_a1', 'L3_gnn_a2']


def kernel(**inputs):
    import numpy as _np
    import concourse.bacc as _bacc
    from concourse import mybir as _mybir
    from concourse.bass_utils import run_bass_kernel_spmd as _run

    nc = _bacc.Bacc("TRN2", target_bir_lowering=False, num_devices=1)
    arrays, aps = {}, {}
    for name in _INS:
        a = _np.ascontiguousarray(inputs[name])
        arrays[f"in_{name}_dram"] = a
        aps[name] = nc.dram_tensor(f"in_{name}_dram", a.shape, _mybir.dt.from_np(a.dtype), kind="ExternalInput").ap()
    out = nc.dram_tensor("out_0_dram", (4096, 256), _mybir.dt.float32, kind="ExternalOutput").ap()
    build(nc, aps, out)
    r = _run(nc, [arrays], core_ids=[0])
    return r.results[0]["out_0_dram"]
```
